# Optimizing a Trainium2 kernel written in Bass

```python
import numpy as np
import jax
import jax.numpy as jnp

def _softmax(x, axis=-1):
    return jax.nn.softmax(x, axis=axis)

def _gelu(x):
    return jax.nn.gelu(x, approximate=True)

def _silu(x):
    return jax.nn.silu(x)

def _sigmoid(x):
    return jax.nn.sigmoid(x)

def _layernorm(x, axis=-1, eps=1e-05):
    m = jnp.mean(x, axis=axis, keepdims=True)
    v = jnp.var(x, axis=axis, keepdims=True)
    return (x - m) / jnp.sqrt(v + eps)

def _scatter_add(tgt, idx, src, axis=0):
    return tgt.at[idx].add(src)

def _segment_sum(src, seg, n):
    return jax.ops.segment_sum(src, seg, n)
kernel_name = 'mk_macaron_d1_jaxref_r2_974712'

def setup_inputs(seed: int=0):
    np.random.seed(seed)
    _w = jnp.asarray

    def _L0_attn_setup():
        import jax, jax.numpy as jnp
        import numpy as np
        B, S, DIM, H = (2, 1024, 512, 16)
        D = DIM // H

        def _xavier(key, shape):
            a = float(np.sqrt(6.0 / (shape[0] + shape[1])))
            return jax.random.uniform(key, shape, minval=-a, maxval=a, dtype=jnp.float32)

        def _split_heads(t):
            b, s, _ = t.shape
            return t.reshape(b, s, H, D).transpose(0, 2, 1, 3).reshape(b * H, s, D)
        key = jax.random.key(seed)
        ks = jax.random.split(key, 8)
        x = jax.random.normal(ks[0], (B, S, DIM), dtype=jnp.float32)
        Wq = _xavier(ks[1], (DIM, DIM))
        Wk = _xavier(ks[2], (DIM, DIM))
        Wv = _xavier(ks[3], (DIM, DIM))
        Wo = _xavier(ks[4], (DIM, DIM))
        bq = jax.random.normal(ks[5], (DIM,), dtype=jnp.float32) * 0.02
        bk = jax.random.normal(ks[6], (DIM,), dtype=jnp.float32) * 0.02
        bv = jax.random.normal(ks[7], (DIM,), dtype=jnp.float32) * 0.02
        bo = jnp.zeros((DIM,), dtype=jnp.float32)
        return {'x': x, 'Wq': Wq, 'bq': bq, 'Wk': Wk, 'bk': bk, 'Wv': Wv, 'bv': bv, 'Wo': Wo, 'bo': bo}
    _L0_attn_in = _L0_attn_setup()

    def _L0_ffn_setup():
        import jax, jax.numpy as jnp
        import numpy as np
        B, S, D, E, H, K = (64, 1024, 512, 32, 2048, 8)
        key = jax.random.key(seed)
        k0, k1, k2, k3 = jax.random.split(key, 4)
        x = jax.random.normal(k0, (B, S, D), jnp.float32)
        gate_w = jax.random.normal(k1, (E, D), jnp.float32) * (1.0 / np.sqrt(D))
        gate_b = jnp.zeros((E,), jnp.float32)
        w1 = jax.random.normal(k2, (E, D + 1, H), jnp.float32) * (1.0 / np.sqrt(D + 1))
        w2 = jax.random.normal(k3, (E, H + 1, D), jnp.float32) * (1.0 / np.sqrt(H + 1))
        return {'x': x, 'gate_w': gate_w, 'gate_b': gate_b, 'w1': w1, 'w2': w2}
    _L0_ffn_in = _L0_ffn_setup()
    _d = {'L0_attn_x': _L0_attn_in['x'], 'L0_attn_Wq': _L0_attn_in['Wq'], 'L0_attn_bq': _L0_attn_in['bq'], 'L0_attn_Wk': _L0_attn_in['Wk'], 'L0_attn_bk': _L0_attn_in['bk'], 'L0_attn_Wv': _L0_attn_in['Wv'], 'L0_attn_bv': _L0_attn_in['bv'], 'L0_attn_Wo': _L0_attn_in['Wo'], 'L0_attn_bo': _L0_attn_in['bo'], 'L0_ffn_gate_w': _L0_ffn_in['gate_w'], 'L0_ffn_gate_b': _L0_ffn_in['gate_b'], 'L0_ffn_w1': _L0_ffn_in['w1'], 'L0_ffn_w2': _L0_ffn_in['w2']}
    _x0 = _d['L0_attn_x']
    _d['L0_attn_x'] = jax.random.normal(jax.random.fold_in(jax.random.key(seed), 1), (8, 1024, 512), dtype=_x0.dtype)
    del _x0
    return _d

def reference(L0_attn_x, L0_attn_Wq, L0_attn_bq, L0_attn_Wk, L0_attn_bk, L0_attn_Wv, L0_attn_bv, L0_attn_Wo, L0_attn_bo, L0_ffn_gate_w, L0_ffn_gate_b, L0_ffn_w1, L0_ffn_w2):

    def _L0_attn_ref(x, Wq, bq, Wk, bk, Wv, bv, Wo, bo):
        import jax, jax.numpy as jnp
        import numpy as np
        B, S, DIM, H = (2, 1024, 512, 16)
        D = DIM // H

        def _xavier(key, shape):
            a = float(np.sqrt(6.0 / (shape[0] + shape[1])))
            return jax.random.uniform(key, shape, minval=-a, maxval=a, dtype=jnp.float32)

        def _split_heads(t):
            b, s, _ = t.shape
            return t.reshape(b, s, H, D).transpose(0, 2, 1, 3).reshape(b * H, s, D)
        b, s, _ = x.shape
        q = _split_heads(x @ Wq.T + bq)
        k = _split_heads(x @ Wk.T + bk)
        v = _split_heads(x @ Wv.T + bv)
        q = jnp.exp(q)
        k = jnp.exp(k)
        kv = jnp.cumsum(k[:, :, :, None] * v[:, :, None, :], axis=1)
        k1 = jnp.cumsum(k, axis=1)
        num = jnp.einsum('zsD,zsDd->zsd', q, kv)
        den = jnp.sum(q * k1, axis=-1, keepdims=True)
        out = num / den
        out = out.reshape(b, H, s, D).transpose(0, 2, 1, 3).reshape(b, s, DIM)
        return out @ Wo.T + bo

    def _L0_ffn_ref(x, gate_w, gate_b, w1, w2):
        import jax, jax.numpy as jnp
        import numpy as np
        B, S, D, E, H, K = (64, 1024, 512, 32, 2048, 8)
        b, s, d = x.shape
        logits = jnp.einsum('bsd,ed->bse', x, gate_w) + gate_b
        probs = jax.nn.softmax(logits, axis=-2)
        vals_t, idx_t = jax.lax.top_k(probs.transpose(0, 2, 1), K)
        vals = vals_t.transpose(0, 2, 1)
        idx = idx_t.transpose(0, 2, 1)
        flat_idx = idx.reshape(b, K * E)
        tok = jnp.take_along_axis(x, flat_idx[:, :, None], axis=1)
        tok = tok.reshape(b, K, E, d)
        merged = jnp.einsum('bked,bke->bed', tok, vals)
        ones = jnp.ones(merged.shape[:-1] + (1,), merged.dtype)
        h = jnp.einsum('bei,eih->beh', jnp.concatenate([merged, ones], -1), w1)
        h = jax.nn.gelu(h, approximate=False)
        o = jnp.einsum('bej,ejo->beo', jnp.concatenate([h, ones], -1), w2)
        out_tok = jnp.einsum('beo,bke->bkeo', o, vals).reshape(b, K * E, d)
        out = jnp.zeros_like(x).at[jnp.arange(b)[:, None], flat_idx].add(out_tok)
        return out
    x = L0_attn_x
    x = x + 0.5 * _L0_ffn_ref(_layernorm(x, axis=-1), L0_ffn_gate_w, L0_ffn_gate_b, L0_ffn_w1, L0_ffn_w2)
    x = x + _L0_attn_ref(_layernorm(x, axis=-1), L0_attn_Wq, L0_attn_bq, L0_attn_Wk, L0_attn_bk, L0_attn_Wv, L0_attn_bv, L0_attn_Wo, L0_attn_bo)
    x = x + 0.5 * _L0_ffn_ref(_layernorm(x, axis=-1), L0_ffn_gate_w, L0_ffn_gate_b, L0_ffn_w1, L0_ffn_w2)
    return x

_drawn_inputs = setup_inputs


def setup_inputs(seed=0):
    import zlib

    import numpy as np

    out = dict(_drawn_inputs(seed))
    spreads = {'L0_attn_bo': (0.0, 0.1), 'L0_ffn_gate_b': (0.0, 2.0)}
    factors = {'L0_attn_bq': 64.0, 'L0_attn_bk': 64.0, 'L0_attn_bv': 2.881}
    for name, (base, spread) in spreads.items():
        noise = np.random.default_rng([zlib.crc32(name.encode()), seed]).standard_normal(out[name].shape)
        drawn = base * np.exp(spread * noise) if base else spread * noise
        out[name] = jnp.asarray(drawn.astype(out[name].dtype))
    for name, factor in factors.items():
        out[name] = (out[name] * factor).astype(out[name].dtype)
    return out
```

```python
import concourse.bass as bass
from concourse import mybir
from contextlib import ExitStack


class Queue:

    def __init__(self, sem):
        self.sem, self.count, self.items = sem, 0, []

    def __call__(self, fn, *waits, inc=True):
        if inc:
            self.count += 1
        self.items.append((waits, fn, (self.sem, 1) if inc else None))
        return (self.sem, self.count)

    def dma(self, counter, out, in_, *waits):
        counter[1] += 16
        self.items.append((waits, lambda e: e.dma_start(out, in_), (counter[0], 16)))
        return (counter[0], counter[1])

    def wait(self, *waits):
        self.items.append((waits, None, None))

    def issue(self, eng):
        seen = {}
        for waits, fn, inc in self.items:
            for w in waits:
                if w is not None and seen.get(id(w[0]), 0) < w[1]:
                    eng.wait_ge(w[0], w[1])
                    seen[id(w[0])] = w[1]
            if fn is not None:
                ins = fn(eng)
                if inc is not None:
                    ins.then_inc(inc[0], inc[1])


def macaron_block(nc, x, Wq, bq, Wk, bk, Wv, bv, Wo, bo, gate_w, gate_b, w1, w2, out):
    F = mybir.dt.float32
    ALU = mybir.AluOpType
    ACT = mybir.ActivationFunctionType
    AX = mybir.AxisListType

    B, S, D, E, H = 8, 1024, 512, 32, 2048
    NT = B * S // 128
    LOWEST = -3.4028234663852886e38
    EPS = 1e-5

    x2d = nc.dram_tensor("x2_scratch", (B, S, D), F).ap()
    xs = x.rearrange("b (c p) d -> (b c) p d", p=128)
    x2s = x2d.rearrange("b (c p) d -> (b c) p d", p=128)
    outs = out.rearrange("b (c p) d -> (b c) p d", p=128)

    ctx = ExitStack()
    with ctx:
        big = ctx.enter_context(nc.sbuf_tensor("big", [128, 57000], F))
        ps = ctx.enter_context(nc.psum_tensor("ps", [128, 8, 512], F))

        def sem(name):
            return ctx.enter_context(nc.semaphore(name))

        class Area:
            def __init__(self, at):
                self.at = at

            def take(self, n):
                self.at += n
                return big[:, self.at - n:self.at]

        a = Area(0)
        ring = [a.take(4096) for _ in range(4)]
        WT = [a.take(2048).rearrange("p (k n) -> p k n", k=4) for _ in range(4)]
        M = [a.take(2048).rearrange("p (h t) -> p h t", h=2) for _ in range(2)]
        OBD = a.take(4096).rearrange("p (b n) -> p b n", b=8)
        MG = a.take(1120).rearrange("p (k c) -> p k c", k=4)
        B1, B2 = a.take(512), a.take(512)
        IDN, TRI, ONES, MBD = (a.take(128) for _ in range(4))
        SEL = a.take(288)
        GT = a.take(128).rearrange("p (k e) -> p k e", k=4)
        BQ, BK, BV, BO = (a.take(512) for _ in range(4))
        SM = a.take(256)
        xn3_at = a.at
        XN3 = [a.take(4096).rearrange("p (c n) -> p c n", c=8) for _ in range(2)]
        XL = [a.take(512) for _ in range(4)]
        XT3 = [a.take(512).rearrange("p (k t) -> p k t", k=4) for _ in range(2)]
        L, LR, EX = (a.take(1024) for _ in range(3))
        MT = a.take(256).rearrange("p (c e) -> p c e", c=8)
        qb_at = a.at
        QB = a.take(2048).rearrange("p (g r t) -> p g r t", g=4, r=4)
        ST = a.take(2048).rearrange("p (g n) -> p g n", g=4)
        assert a.at <= 57000

        s = Area(4096)
        KT, QH, QT, AT, KV, TMP, KS, PR = (s.take(512) for _ in range(8))
        X1 = [s.take(512) for _ in range(4)]
        X2 = [s.take(512) for _ in range(2)]
        XN = [s.take(512) for _ in range(2)]
        XT = [s.take(512).rearrange("p (k t) -> p k t", k=4) for _ in range(2)]
        Qs = [s.take(512) for _ in range(2)]
        Ks = [s.take(512) for _ in range(2)]
        Vs = [s.take(512) for _ in range(2)]
        assert s.at == 16384

        f = Area(xn3_at)
        HG = [f.take(512) for _ in range(2)]
        HT = [f.take(512) for _ in range(2)]
        PT = [f.take(512) for _ in range(2)]
        wst = Area(qb_at)
        WST = [wst.take(2048).rearrange("p (k n) -> p k n", k=4) for _ in range(2)]
        GW = WST[0][0:32, 0, :]
        fx = Area(4 * 4096)
        FX = [fx.take(512) for _ in range(16)]

        ST6 = [SM[:, 8 * i:8 * i + 6] for i in range(2)]
        MV = [SM[:, 16 + 4 * i:18 + 4 * i] for i in range(2)]
        VE = [SM[:, 24 + i:25 + i] for i in range(2)]
        RS = [SM[:, 26 + i:27 + i] for i in range(2)]
        NHALF = SM[:, 28:29]
        GB = SM[:, 29:30]
        T8 = SM[:, 32:40]
        NMX = SM[:, 40:41]
        SUM = SM[:, 41:42]
        RSUM = SM[:, 42:43]
        DEN = SM[:, 48:64]
        RDEN = SM[:, 64:80]

        pe, dve, act, pool = (Queue(sem(n)) for n in ("s_pe", "s_dve", "s_act", "s_pool"))
        sp = Queue(sem("s_sp"))

        def counter(name):
            return [sem(name), 0]

        c_ring = [counter(f"c_ring{i}") for i in range(4)]
        c_x = [counter(f"c_x{i}") for i in range(4)]
        c_x2 = [counter(f"c_x2{i}") for i in range(2)]
        c_fl = [counter(f"c_fl{i}") for i in range(16)]
        c_fs = [counter(f"c_fs{i}") for i in range(16)]
        c_wst = [counter(f"c_wst{i}") for i in range(2)]
        c_b1, c_b2, c_bias, c_gb, c_gw = (counter(n) for n in ("c_b1", "c_b2", "c_bias", "c_gb", "c_gw"))

        free = [None] * 8

        def mm(o, l, r, start, stop):
            return lambda e: nc.tensor.matmul(o, l, r, start=start, stop=stop, skip_group_check=True)

        def tr(o, i, n=128):
            return lambda e: nc.tensor.transpose(o, i, IDN[0:n, 0:n])

        def copy_act(o, i):
            return lambda e: nc.scalar.copy(o, i)

        def tt(o, p, q, op):
            return lambda e: nc.vector.tensor_tensor(o, p, q, op)

        def const(o, v):
            return pool(lambda e: nc.gpsimd.memset(o, v), (pool.sem, pool.count))

        const(IDN, 0.0)
        const(TRI, 1.0)
        const(ONES, 1.0)
        const(MBD, 0.0)
        const(SEL, 0.0)
        const(NHALF, -0.5)
        const(MG[:, :, 256:280], 0.0)

        def select(t, pattern, cm, base, op, fill):
            return pool(lambda e: nc.gpsimd.affine_select(out=t, in_=t, compare_op=op, fill=fill, base=base,
                                                          pattern=pattern, channel_multiplier=cm),
                        (pool.sem, pool.count))

        t_idn = select(IDN, [[-1, 128]], 1, 0, ALU.not_equal, 1.0)
        select(TRI, [[1, 128]], -1, 0, ALU.is_ge, 0.0)
        for r in range(4):
            t_cst = pool(lambda e, r=r: nc.gpsimd.memset(MBD[32 * r:32 * r + 32, 32 * r:32 * r + 32], 1.0),
                         (pool.sem, pool.count))
        for j in range(4):
            t_cst = select(SEL[:, 0:287], [[-1, 287]], 32, 31 - 1024 * j, ALU.not_equal, 1.0)
        t_obd0 = pool(lambda e: nc.gpsimd.memset(big[:, 28672:32768], 0.0), (pool.sem, pool.count))
        assert 4 * 4096 + 4 * 2048 + 2 * 2048 == 28672

        ring_tok, ring_free = {}, [None] * 4

        def load_chunk(g, *waits):
            e, part = (g // 4) % E, g % 4
            slot = g % 4
            if part < 2:
                src = w1[e, 0:512, :].rearrange("(p k) n -> p k n", k=4)[:, 2 * part:2 * part + 2, :]
                dst = ring[slot].rearrange("p (k n) -> p k n", k=2)
            else:
                src = w2[e, 0:2048, :].rearrange("(j c i) n -> c j (i n)", j=4, i=4)[:, 2 * part - 4:2 * part - 2, :]
                dst = ring[slot].rearrange("p (j n) -> p j n", j=2)
            ring_tok[g] = sp.dma(c_ring[slot], dst, src, ring_free[slot], *waits)

        ln_n = [0]

        def norm(src, dst, src_tok, *dst_waits):
            i = ln_n[0] % 2
            ln_n[0] += 1
            t = dve(lambda e: nc.vector.bn_stats(ST6[i], src), src_tok)
            t = dve(lambda e: nc.vector.bn_aggr(MV[i], ST6[i]), t)
            t = dve(lambda e: nc.vector.tensor_scalar(VE[i], MV[i][:, 1:2], EPS, None, ALU.add), t)
            t = pool(lambda e: nc.gpsimd.tensor_tensor(RS[i], VE[i], NHALF, ALU.pow), t)
            return dve(lambda e: nc.vector.tensor_scalar(dst, src, MV[i][:, 0:1], RS[i], ALU.subtract, ALU.mult),
                       t, *dst_waits)

        turn = [0]

        def bank():
            turn[0] += 1
            return turn[0] % 3

        xt3_free = [None, None]
        logit_tok = {}
        mt_free = [None]
        l_free = [None] * 4
        xt3_tok = {}

        def gate_transpose(n, src, tok):
            k = bank()
            for j in range(4):
                t = pe(tr(ps[:, k, 128 * j:128 * j + 128], src[:, 128 * j:128 * j + 128]),
                       tok, free[k], t_idn, inc=j == 3)
            i = n % 2
            free[k] = xt3_tok[n] = act(copy_act(XT3[i], ps[:, k, :].rearrange("p (k t) -> p k t", k=4)),
                                       t, xt3_free[i])

        def gate_logits(n):
            b, c, i = n // 8, n % 8, n % 2
            q = 32 * (b % 4)
            k = bank()
            for j in range(4):
                t = pe(mm(ps[q:q + 32, k, 0:128], GT[:, j, :], XT3[i][:, j, :], j == 0, j == 3),
                       xt3_tok[n], free[k], t_gt, inc=j == 3)
            xt3_free[i] = t
            free[k] = logit_tok[n] = act(
                lambda e: nc.scalar.activation(L[q:q + 32, 128 * c:128 * c + 128], ps[q:q + 32, k, 0:128],
                                               ACT.Identity, bias=GB[q:q + 32, :]), t, t_gb, l_free[b % 4])

        def topk(b, m):
            q = 32 * (b % 4)
            R = slice(q, q + 32)
            t = dve(lambda e: nc.vector.max(T8[R, :], L[R, :]), logit_tok[8 * b + 7])
            t2 = dve(lambda e: nc.vector.match_replace(LR[R, :], T8[R, :], L[R, :], LOWEST), t)
            t = dve(lambda e: nc.vector.tensor_scalar(NMX[R, :], T8[R, 0:1], -1.0, None, ALU.mult), t)
            t = act(lambda e: nc.scalar.activation(EX[R, :], L[R, :], ACT.Exp, bias=NMX[R, :],
                                                   accum_out=SUM[R, :]), t, pr3_free[0])
            ts = dve(lambda e: nc.vector.reciprocal(RSUM[R, :], SUM[R, :]), t)
            t2 = dve(tt(LR[R, :], L[R, :], LR[R, :], ALU.not_equal), t2)
            l_free[b % 4] = t2
            return dve(lambda e: nc.vector.scalar_tensor_tensor(
                out=M[m][R, b // 4, :], in0=EX[R, :], scalar=RSUM[R, :], in1=LR[R, :],
                op0=ALU.mult, op1=ALU.mult), ts, t2)

        def merge(b, m, tok, xn_tok):
            q = 32 * (b % 4)
            k = bank()
            for c in range(8):
                t = pe(lambda e, c=c, k=k: nc.tensor.transpose(ps[:, k, 32 * c:32 * c + 32],
                                                          M[m][q:q + 32, b // 4, 128 * c:128 * c + 128],
                                                          IDN[q:q + 32, q:q + 32]), tok, free[k], inc=c == 7)
            free[k] = t = act(copy_act(MT, ps[:, k, 0:256].rearrange("p (c e) -> p c e", c=8)), t, mt_free[0])
            k = bank()
            for h in range(2):
                for c in range(4):
                    t2 = pe(mm(ps[32 * c:32 * c + 32, k, :], MT[:, 4 * h + c, :], XN3[b % 2][:, 4 * h + c, :],
                               h == 0, h == 1), t, xn_tok, free[k], inc=h == 1 and c == 3)
            mt_free[0] = t2
            free[k] = t = act(copy_act(PR3, ps[:, k, :]), t2, pr3_free[0])
            k = bank()
            for j in range(4):
                t = pe(tr(ps[:, k, 128 * j:128 * j + 128], PR3.rearrange("p (c k) -> p k c", k=4)[:, j, :]),
                       t, free[k], inc=j == 3)
            pr3_free[0] = t
            free[k] = mg_tok[b] = dve(lambda e: nc.vector.tensor_reduce(
                MG[:, :, 0:256].rearrange("p k (e b) -> p k e b", b=8)[:, :, :, b],
                ps[:, k, :].rearrange("p (k q e) -> p k e q", k=4, q=4), AX.X, ALU.add), t, mg_free[0])
            return t2

        PR3 = EX[:, 0:512]
        pr3_free = [None]
        mg_tok, mg_free = {}, [None]

        t_gw = sp.dma(c_gw, GW, gate_w)
        for r in range(4):
            t_gb = sp.dma(c_gb, GB[32 * r:32 * r + 32, :], gate_b.rearrange("(e a) -> e a", a=1))
        xl_tok, xl_free = {}, [None] * 4

        def load_x(n):
            xl_tok[n] = sp.dma(c_x[n % 4], XL[n % 4], xs[n], xl_free[n % 4])

        for n in range(4):
            load_x(n)
        k = bank()
        for j in range(4):
            t = pe(lambda e, j=j, k=k: nc.tensor.transpose(ps[:, k, 32 * j:32 * j + 32], GW[:, 128 * j:128 * j + 128],
                                                      IDN[0:32, 0:32]), t_gw, t_idn, inc=j == 3)
        free[k] = t_gt = act(copy_act(GT, ps[:, k, 0:128].rearrange("p (k e) -> p k e", k=4)), t)

        xn_free = [None, None]
        xn_tok = {}
        pend = {}
        for n in range(NT + 4):
            if n < NT:
                b, c = n // 8, n % 8
                xn_tok[n] = xl_free[n % 4] = norm(XL[n % 4], XN3[b % 2][:, c, :], xl_tok[n], xn_free[b % 2])
                if n + 4 < NT:
                    load_x(n + 4)
                if n % 16 == 8 and n < 64:
                    load_chunk(n // 16)
                gate_transpose(n, XN3[b % 2][:, c, :], xn_tok[n])
            if 1 <= n <= NT:
                gate_logits(n - 1)
            if n >= 8 and n % 8 == 1:
                pend[n // 8 - 1] = topk(n // 8 - 1, 0)
            if n >= 8 and n % 8 == 3:
                b = n // 8 - 1
                xn_free[b % 2] = merge(b, 0, pend[b], xn_tok[8 * b + 7])

        def experts(first, extra):
            hb, tb, pb = {}, {}, {}
            h_tok, hg_tok, ht_tok, pt_tok, hgf, htf, ptf = {}, {}, {}, {}, [None] * 2, [None] * 2, [None] * 2
            o_last = None
            for e in range(E + 1):
                if e < E:
                    g = first + 4 * e
                    i = e % 2
                    k = i
                    for j in range(4):
                        r = 32 * j + e
                        pe(mm(ps[32 * j:32 * j + 32, k, :], IDN[:, r:r + 1].broadcast_to([128, 32]), B1,
                              True, False), free[k], t_b1, mg_tok[7], inc=False)
                    for kt in range(4):
                        v = ring[(g + kt // 2) % 4].rearrange("p (k n) -> p k n", k=2)
                        for j in range(4):
                            t = pe(mm(ps[32 * j:32 * j + 32, k, :], MG[:, kt, 8 * e:8 * e + 32],
                                      v[:, kt % 2, 512 * j:512 * j + 512], False, kt == 3),
                                   ring_tok[g + kt // 2], inc=kt % 2 == 1 and j == 3)
                        if kt % 2 == 1:
                            slot = (g + kt // 2) % 4
                            ring_free[slot] = t
                            if g + kt // 2 + 4 < first + 128:
                                load_chunk(g + kt // 2 + 4)
                    mg_free[0] = t
                    free[k] = t = act(lambda q, i=i, k=k: nc.scalar.activation(HG[i], ps[:, k, :], ACT.Gelu),
                                      t, hgf[i])
                    hg_tok[e] = t
                if e >= 1:
                    p = e - 1
                    i = p % 2
                    for half in range(2):
                        off = 128 * half + 31 - p
                        t = pe(mm(ps[:, 6 + half, :], SEL[:, off:off + 128], PT[i], p == 0, p == E - 1),
                               pt_tok[p], free[6 + half], t_cst)
                    ptf[i] = o_last = t
                if e < E:
                    i = e % 2
                    k = 2 + i
                    for q in range(4):
                        t = pe(tr(ps[:, k, 128 * q:128 * q + 128],
                                  HG[i].rearrange("p (c t) -> p t c", t=4)[:, q, :]),
                               hg_tok[e], free[k], inc=q == 3)
                    hgf[i] = t
                    free[k] = t = dve(lambda q, i=i, k=k: nc.vector.tensor_copy(HT[i], ps[:, k, :]), t, htf[i])
                    k = 4 + i
                    for j in range(4):
                        v = ring[(g + 2 + j // 2) % 4].rearrange("p (j i n) -> p j i n", j=2, i=4)
                        for q in range(4):
                            t2 = pe(mm(ps[32 * q:32 * q + 32, k, :], HT[i][:, 128 * q + 32 * j:128 * q + 32 * j + 32],
                                       v[:, j % 2, q, :], j == 0, j == 3),
                                    t, free[k], ring_tok[g + 2 + j // 2], inc=j % 2 == 1 and q == 3)
                        if j % 2 == 1:
                            slot = (g + 2 + j // 2) % 4
                            ring_free[slot] = t2
                            if g + 2 + j // 2 + 4 < first + 128:
                                load_chunk(g + 2 + j // 2 + 4)
                    htf[i] = t2
                    free[k] = pt_tok[e] = act(copy_act(PT[i], ps[:, k, :]), t2, ptf[i])
                    extra(e)
            toks = []
            for b in range(B):
                q = 32 * (b % 4)
                R = slice(q, q + 32)
                toks.append(dve(tt(OBD[R, b, :], ps[R, 6 + b // 4, :], B2[R, :], ALU.add), o_last, t_b2, t_obd0,
                                obd_free[0]))
            free[6] = free[7] = toks[-1]
            return toks

        obd_free = [None]
        for j in range(4):
            t_b1 = sp.dma(c_b1, B1[32 * j:32 * j + 32, :], w1[:, 512, 512 * j:512 * j + 512])
            t_b2 = sp.dma(c_b2, B2[32 * j:32 * j + 32, :], w2[:, 2048, :])
        for t_, s_ in ((BQ, bq), (BK, bk), (BV, bv), (BO, bo)):
            t_bias = sp.dma(c_bias, t_, s_.partition_broadcast(128))

        wt_tok = [None] * 4
        wst_free = [t_gt, None]
        wst_tok = {}

        def prepare(e):
            if e % 6 == 0 and e < 24:
                m = e // 6
                wst_tok[m] = act.dma(c_wst[m % 2], WST[m % 2],
                                     (Wq, Wk, Wv, Wo)[m].rearrange("(o p) i -> p o i", p=128), wst_free[m % 2])
            m, kt = e // 6, e % 6 - 1
            if 0 <= kt < 4 and m < 4:
                k = 6 - 6 + 2 + (e + 1) % 2
                for o in range(4):
                    t = pe(tr(ps[:, k, 128 * o:128 * o + 128], WST[m % 2][:, o, 128 * kt:128 * kt + 128]),
                           wst_tok[m], free[k], inc=o == 3)
                wst_free[m % 2] = t
                free[k] = wt_tok[m] = act(copy_act(WT[m][:, kt, :], ps[:, k, :]), t)

        o_tok = experts(0, prepare)
        t_w = wt_tok[3]

        x1_tok, x1b_tok, x2_tok, xnt_tok, xt_tok = {}, {}, {}, {}, {}
        q_tok, k_tok, v_tok = {}, {}, {}
        x1_free, x2_free, xnf, xtf = [None] * 4, [None] * 2, [None] * 2, [None] * 2
        kf, vf = [[], []], [[], []]
        once = {n_: None for n_ in ("KT", "QH", "QT", "QB", "AT", "KV", "TMP", "KS", "ST")}
        kv_tok = ks_tok = None
        z_qb = pool(lambda e: nc.gpsimd.memset(QB, 0.0), wst_free[0], wst_free[1])
        done1 = ring_free[3]

        def residual(n):
            b, c = n // 8, n % 8
            k = bank()
            t = pe(mm(ps[:, k, :], M[0][:, b // 4, 128 * c:128 * c + 128], OBD[:, b, :], True, True),
                   free[k], o_tok[b], o_tok[7])
            obd_free[0] = t
            i, j = n % 4, n % 2
            free[k] = xl_free[i] = x1_tok[n] = dve(
                lambda e: nc.vector.scalar_tensor_tensor(out=X1[i], in0=ps[:, k, :], scalar=0.5, in1=XL[i],
                                                         op0=ALU.mult, op1=ALU.add), t, xl_tok[NT + n], x1_free[i])
            xnt_tok[n] = norm(X1[i], XN[j], x1_tok[n], xnf[j])
            x1b_tok[n] = pool(lambda e: nc.gpsimd.tensor_tensor(X1[i], X1[i], BO, ALU.add), xnt_tok[n], t_bias)

        def load_x1(n):
            i = n % 4
            xl_tok[NT + n] = sp.dma(c_x[i], XL[i], xs[n], xl_free[i])

        def x_transpose(n):
            k, i = bank(), n % 2
            for j in range(4):
                t = pe(tr(ps[:, k, 128 * j:128 * j + 128], XN[i][:, 128 * j:128 * j + 128]),
                       xnt_tok[n], free[k], inc=j == 3)
            xnf[i] = t
            free[k] = xt_tok[n] = act(copy_act(XT[i], ps[:, k, :].rearrange("p (k t) -> p k t", k=4)), t, xtf[i])

        def project(n, w, dst, bias, exp, waits):
            k, i = bank(), n % 2
            for j in range(4):
                t = pe(mm(ps[:, k, :], XT[i][:, j, :], WT[w][:, j, :], j == 0, j == 3),
                       xt_tok[n], free[k], t_w, inc=j == 3)
            if w == 2:
                xtf[i] = t
            free[k] = t = dve(tt(dst, ps[:, k, :], bias, ALU.add), t, t_bias, *waits)
            if exp:
                t = act(lambda e: nc.scalar.activation(dst, dst, ACT.Exp), t)
            return t

        def h4(t):
            return t.rearrange("p (g n) -> p g n", g=4)

        for n in range(4):
            load_x1(n)
        load_chunk(128)
        last_x2_store = [None] * 2
        for n in range(-3, NT + 4):
            live = 0 <= n < NT
            nxt = 0 <= n + 1 < NT
            if live:
                b, c, i = n // 8, n % 8, n % 2
                k = bank()
                t = pe(mm(ps[:, k, :], TRI, Ks[i], True, c == 0), k_tok[n], free[k], inc=c == 0)
                if c:
                    t = pe(mm(ps[:, k, :], ONES, KS, False, True), ks_tok)
                kc = t
                free[k] = t = dve(tt(PR, ps[:, k, :], Qs[i], ALU.mult), t, q_tok[n])
                t = dve(lambda e: nc.vector.tensor_reduce(DEN, PR.rearrange("p (h d) -> p h d", h=16),
                                                          AX.X, ALU.add), t)
                t = dve(lambda e: nc.vector.reciprocal(RDEN, DEN), t)
                qh_tok = dve(tt(QH.rearrange("p (h d) -> p h d", h=16), Qs[i].rearrange("p (h d) -> p h d", h=16),
                                RDEN.unsqueeze(2).broadcast_to([128, 16, 32]), ALU.mult), t, once["QH"])
                if c == 0:
                    ks_tok = pool(lambda e, i=i: nc.gpsimd.tensor_copy(KS, Ks[i]), kc)
                elif c < 7:
                    ks_tok = pool(lambda e, i=i: nc.gpsimd.tensor_tensor(KS, KS, Ks[i], ALU.add), kc)
                kf[i] = [ks_tok]
                k = bank()
                for g in range(4):
                    t = pe(tr(ps[:, k, 128 * g:128 * g + 128], Ks[i][:, 128 * g:128 * g + 128]), free[k], k_tok[n],
                           inc=g == 3)
                free[k] = kt_tok = act(copy_act(KT, ps[:, k, :]), t, once["KT"])
            if nxt:
                q_tok[n + 1] = project(n + 1, 0, Qs[(n + 1) % 2], BQ, True, [])
            if live:
                k = bank()
                for g in range(4):
                    t = pe(tr(ps[:, k, 128 * g:128 * g + 128], QH[:, 128 * g:128 * g + 128]), free[k], qh_tok,
                           inc=g == 3)
                once["QH"] = t
                for r in range(4):
                    R = slice(32 * r, 32 * r + 32)
                    tq = act(copy_act(QB[R, :, r, :], ps[R, k, :].rearrange("p (g t) -> p g t", g=4)),
                             t, once["QB"], z_qb)
                free[k] = qt_tok = act(copy_act(QT, ps[:, k, :]), t, once["QT"])
            if nxt:
                k_tok[n + 1] = project(n + 1, 1, Ks[(n + 1) % 2], BK, True, kf[(n + 1) % 2])
            if live:
                s_tok = []
                for g in range(4):
                    s_tok.append(pe(mm(ps[:, 4 + g, :], h4(KT)[:, g, :], QB[:, g, :, :], True, True),
                                    free[4 + g], kt_tok, tq))
                once["KT"] = once["QB"] = s_tok[3]
                for g in range(4):
                    free[4 + g] = st_tok = dve(tt(h4(ST[:, g, :]), h4(ps[:, 4 + g, :]),
                                                  TRI.unsqueeze(1).broadcast_to([128, 4, 128]), ALU.mult),
                                               s_tok[g], once["ST"])
            if nxt:
                v_tok[n + 1] = project(n + 1, 2, Vs[(n + 1) % 2], BV, False, vf[(n + 1) % 2])
            if live:
                for g in range(4):
                    if c:
                        ti = pe(mm(ps[:, 3, 128 * g:128 * g + 128], h4(KV)[:, g, :], h4(QT)[:, g, :], True, False),
                                free[3], kv_tok, qt_tok, inc=g == 3)
                    for r in range(4):
                        o = ps[32 * r:32 * r + 32, 3, 128 * g:128 * g + 128]
                        t = pe(mm(o, Vs[i][:, 128 * g + 32 * r:128 * g + 32 * r + 32],
                                  ST[:, g, 128 * r:128 * r + 128], c == 0, True), free[3], st_tok, v_tok[n],
                               inc=g == 3 and r == 3)
                once["ST"] = once["QT"] = t
                if c:
                    once["KV"] = ti
                free[3] = at_tok = act(copy_act(AT, ps[:, 3, :]), t, once["AT"])
                if c < 7:
                    k = bank()
                    for g in range(4):
                        t = pe(mm(ps[:, k, 128 * g:128 * g + 128], Ks[i][:, 128 * g:128 * g + 128],
                                  Vs[i][:, 128 * g:128 * g + 128], True, True), free[k], inc=g == 3)
                    if c == 0:
                        free[k] = kv_tok = dve(tt(h4(KV), h4(ps[:, k, :]),
                                                  MBD.unsqueeze(1).broadcast_to([128, 4, 128]), ALU.mult),
                                               t, once["KV"])
                    else:
                        free[k] = tm = dve(tt(h4(TMP), h4(ps[:, k, :]),
                                              MBD.unsqueeze(1).broadcast_to([128, 4, 128]), ALU.mult),
                                           t, once["TMP"])
                        kv_tok = once["TMP"] = pool(lambda e: nc.gpsimd.tensor_tensor(KV, KV, TMP, ALU.add),
                                                    tm, once["KV"])
                kf[i] = kf[i] + [t]
                vf[i] = [t]
            if 0 <= n + 2 < NT:
                residual(n + 2)
                if n + 6 < NT:
                    load_x1(n + 6)
            if 1 <= n <= NT:
                gate_transpose(n - 1, XN3[((n - 1) // 8) % 2][:, (n - 1) % 8, :], xn_tok[n - 1])
            if live:
                k = bank()
                for g in range(4):
                    t = pe(mm(ps[:, k, :], h4(AT)[:, g, :], WT[3][:, g, :], g == 0, g == 3), free[k], at_tok,
                           inc=g == 3)
                once["AT"] = t
                j = n % 4
                free[k] = x1_free[j] = t = dve(tt(X2[i], ps[:, k, :], X1[j], ALU.add), t, x1b_tok[n], x2_free[i])
                x2_tok[n] = sp.dma(c_x2[i], x2s[n], X2[i], t)
                xn_tok[n] = norm(X2[i], XN3[b % 2][:, c, :], t, xn_free[b % 2] if c == 0 else None)
                x2_free[i] = x2_tok[n]
            if 0 <= n + 2 < NT:
                x_transpose(n + 2)
            if 1 <= n <= NT:
                gate_logits(n - 1)
            if n >= 8 and n % 8 == 1:
                pend[n // 8 - 1] = topk(n // 8 - 1, 1)
            if n >= 8 and n % 8 == 3:
                bb = n // 8 - 1
                xn_free[bb % 2] = merge(bb, 1, pend[bb], xn_tok[8 * bb + 7])

        att_done = (pe.sem, pe.count)
        act_done, dve_done, pool_done = (act.sem, act.count), (dve.sem, dve.count), (pool.sem, pool.count)
        for g in range(129, 132):
            load_chunk(g, att_done, act_done, dve_done, pool_done, x2_free[0], x2_free[1])
        fl_tok = {}

        def load_f(n):
            fl_tok[n] = sp.dma(c_fl[n % 16], FX[n % 16], x2s[n], fs_tok.get(n - 16), att_done)

        fs_tok = {}

        def reload(e):
            if e >= 16:
                load_f(e - 16)

        o_tok = experts(128, reload)
        for n in range(NT):
            b, c, i = n // 8, n % 8, n % 16
            k = n % 6
            t = pe(mm(ps[:, k, :], M[1][:, b // 4, 128 * c:128 * c + 128], OBD[:, b, :], True, True),
                   free[k], o_tok[b], o_tok[7])
            free[k] = t = dve(lambda e, i=i, k=k: nc.vector.scalar_tensor_tensor(
                out=FX[i], in0=ps[:, k, :], scalar=0.5, in1=FX[i], op0=ALU.mult, op1=ALU.add), t, fl_tok[n])
            fs_tok[n] = sp.dma(c_fs[i], outs[n], FX[i], t)
            if n >= 4 and n + 12 < NT:
                load_f(n + 12)
        sp.wait(*[fs_tok[n] for n in range(NT - 16, NT)])

        block = ctx.enter_context(nc.Block())

        @block.sync
        def _(eng):
            sp.issue(eng)

        @block.gpsimd
        def _(eng):
            pool.issue(eng)

        @block.scalar
        def _(eng):
            act.issue(eng)

        @block.vector
        def _(eng):
            dve.issue(eng)

        @block.tensor
        def _(eng):
            pe.issue(eng)


_INS = ["x", "Wq", "bq", "Wk", "bk", "Wv", "bv", "Wo", "bo"]
_FFN = ["gate_w", "gate_b", "w1", "w2"]


def kernel(**inputs):
    import numpy as _np
    import concourse.bacc as _bacc
    from concourse import mybir as _mybir
    from concourse.bass_utils import run_bass_kernel_spmd as _run

    nc = _bacc.Bacc("TRN2", target_bir_lowering=False, num_devices=1, dynamic_dma_scratch_size=1024)
    arrays, args = {}, []
    for name in ["L0_attn_" + n for n in _INS] + ["L0_ffn_" + n for n in _FFN]:
        a = _np.ascontiguousarray(inputs[name])
        arrays[f"in_{name}"] = a
        args.append(nc.dram_tensor(f"in_{name}", a.shape, _mybir.dt.from_np(a.dtype), kind="ExternalInput").ap())
    out = nc.dram_tensor("out_x", (8, 1024, 512), _mybir.dt.float32, kind="ExternalOutput").ap()
    macaron_block(nc, *args, out)
    r = _run(nc, [arrays], core_ids=[0])
    return r.results[0]["out_x"]
```

```python
import concourse.bass as bass
from concourse import mybir
from contextlib import ExitStack


class Queue:

    def __init__(self, sem):
        self.sem, self.count, self.items = sem, 0, []

    def __call__(self, fn, *waits, inc=True):
        if inc:
            self.count += 1
        self.items.append((waits, fn, (self.sem, 1) if inc else None))
        return (self.sem, self.count)

    def dma(self, counter, out, in_, *waits):
        counter[1] += 16
        self.items.append((waits, lambda e: e.dma_start(out, in_), (counter[0], 16)))
        return (counter[0], counter[1])

    def wait(self, *waits):
        self.items.append((waits, None, None))

    def issue(self, eng):
        seen = {}
        for waits, fn, inc in self.items:
            for w in waits:
                if w is not None and seen.get(id(w[0]), 0) < w[1]:
                    eng.wait_ge(w[0], w[1])
                    seen[id(w[0])] = w[1]
            if fn is not None:
                ins = fn(eng)
                if inc is not None:
                    ins.then_inc(inc[0], inc[1])


def macaron_block(nc, x, Wq, bq, Wk, bk, Wv, bv, Wo, bo, gate_w, gate_b, w1, w2, out):
    F = mybir.dt.float32
    R = mybir.dt.float32r
    ALU = mybir.AluOpType
    ACT = mybir.ActivationFunctionType
    AX = mybir.AxisListType

    B, S, D, E, H = 8, 1024, 512, 32, 2048
    NT = B * S // 128
    LOWEST = -3.4028234663852886e38
    EPS = 1e-5

    wl = nc.dram_tensor("wl_scratch", (4, 4, 128, D), F).ap()
    x2d = nc.dram_tensor("x2_scratch", (B, S, D), F).ap()
    xs = x.rearrange("b (c p) d -> (b c) p d", p=128)
    x2s = x2d.rearrange("b (c p) d -> (b c) p d", p=128)
    outs = out.rearrange("b (c p) d -> (b c) p d", p=128)

    ctx = ExitStack()
    with ctx:
        SIZE = 57040
        CUT = 38272
        big = ctx.enter_context(nc.sbuf_tensor("big", [128, CUT], F))
        big2 = ctx.enter_context(nc.sbuf_tensor("big2", [128, SIZE - CUT], F))
        base = nc.sbuf_base - 4 * SIZE
        ps = ctx.enter_context(nc.psum_tensor("ps", [128, 8, 512], F))

        def sem(name):
            return ctx.enter_context(nc.semaphore(name))

        class Area:
            def __init__(self, at):
                self.at = at

            def take(self, n):
                self.at += n
                assert self.at <= CUT or self.at - n >= CUT
                return big[:, self.at - n:self.at] if self.at <= CUT else big2[:, self.at - n - CUT:self.at - CUT]

        a = Area(0)
        ring = [a.take(4096) for _ in range(4)]
        wth_at = a.at
        a.take(8192)
        m_at = a.at
        M = [a.take(2048).rearrange("p (h t) -> p h t", h=2) for _ in range(2)]
        obd_at = a.at
        OBD = a.take(4096).rearrange("p (b n) -> p b n", b=8)
        MG = a.take(1120).rearrange("p (k c) -> p k c", k=4)
        B1, B2 = a.take(512), a.take(512)
        IDN, TRI, MBD = (a.take(128) for _ in range(3))
        tri_at = a.at
        a.take(256)
        SEL = a.take(288)
        GT = a.take(128).rearrange("p (k e) -> p k e", k=4)
        BQ, BK, BV, BO = (a.take(512) for _ in range(4))
        SM = a.take(256)
        xn3_at = a.at
        NX = 12
        XN3 = [a.take(512) for _ in range(NX)]
        XL = [a.take(512) for _ in range(2)]
        XT3 = [a.take(512).rearrange("p (k t) -> p k t", k=4) for _ in range(2)]
        L = a.take(1024)
        MT = a.take(256).rearrange("p (c e) -> p c e", c=8)
        PR3 = a.take(512)
        qb_at = a.at
        QB = a.take(2048).rearrange("p (g r t) -> p g r t", g=4, r=4)
        ST = a.take(2048).rearrange("p (g n) -> p g n", g=4)
        KT, QH, QT, KV, TMP = (a.take(512) for _ in range(5))
        kh_at = a.at
        a.take(1024)
        ath_at = a.at
        a.take(1024)
        assert a.at <= SIZE

        assert xn3_at == CUT

        s = Area(8192)
        PR = s.take(512)
        X1 = [s.take(512) for _ in range(3)]
        X2, XN = s.take(512), s.take(512)
        xt_at = s.at
        s.take(2048)
        Qs = [s.take(512) for _ in range(2)]
        k_at = s.at
        s.take(1024)
        Vs = [s.take(512) for _ in range(2)]
        assert s.at == 16384

        def halves(name, at, n, dt=R):
            return nc.alloc_sbuf_tensor_at(name, [128, n], dt, offset=base + 4 * at)

        WTH = [halves(f"wth{m}", wth_at + 2048 * m, 2048)[:, :].rearrange("p (k n) -> p k n", k=4) for m in range(4)]
        WTL = [halves(f"wtl{m}", 2048 * m, 2048)[:, :].rearrange("p (k n) -> p k n", k=4) for m in range(4)]
        XTH = [halves(f"xth{i}", xt_at + 512 * i, 512)[:, :].rearrange("p (k t) -> p k t", k=4) for i in range(2)]
        XTL = [halves(f"xtl{i}", xt_at + 1024 + 512 * i, 512)[:, :].rearrange("p (k t) -> p k t", k=4)
               for i in range(2)]
        ATH, ATL = (halves(f"at{i}", ath_at + 512 * i, 512)[:, :] for i in range(2))
        Ks = [halves(f"keys{i}", k_at + 512 * i, 512, F)[:, :] for i in range(2)]
        KH, KL = (halves(f"kh{i}", kh_at + 512 * i, 512)[:, :] for i in range(2))
        UPTO, AFTER = (halves(f"tri{i}", tri_at + 128 * i, 128)[:, :] for i in range(2))

        f = Area(xn3_at)
        HG = [f.take(512) for _ in range(2)]
        HT = [f.take(512) for _ in range(2)]
        PT = [f.take(512) for _ in range(2)]
        WLS = [halves(f"wls{i}", f.at + 512 * i, 512)[:, :] for i in range(2)]
        wst = Area(qb_at)
        WST = [wst.take(2048).rearrange("p (k n) -> p k n", k=4) for _ in range(2)]
        GW = WST[0][0:32, 0, :]
        fx = Area(wth_at)
        FX = [fx.take(512) for _ in range(20)]
        XT4 = [big[:, obd_at + 2048 * i:obd_at + 2048 * i + 2048].rearrange("p (k t) -> p k t", k=4) for i in range(2)]
        fx = Area(qb_at)
        FX += [fx.take(512) for _ in range(8)]
        NF = len(FX)
        XLA = [t[:, at:at + 2048].rearrange("p (t d) -> p t d", t=4)
               for t, at in [(big, wth_at + 2048 * i) for i in range(4)] + [(big2, 2048 * i) for i in range(3)]
               + [(big2, qb_at - CUT), (big2, qb_at + 2048 - CUT)]]
        NX4 = len(XLA)
        TILES = [[XLA[n // 4][:, n % 4, :] for n in range(4 * NX4)], XN3]

        ST6 = [SM[:, 8 * i:8 * i + 6] for i in range(4)]
        MV = [SM[:, 32 + 4 * i:34 + 4 * i] for i in range(4)]
        VE = [SM[:, 48 + i:49 + i] for i in range(4)]
        RS = [SM[:, 52 + i:53 + i] for i in range(4)]
        NHALF = SM[:, 56:57]
        GB = SM[:, 57:58]
        T8 = SM[:, 64:72]
        NMX = SM[:, 72:73]
        SUM = SM[:, 73:74]
        RSUM = SM[:, 74:75]
        DEN = SM[:, 80:96]
        RDEN = SM[:, 96:112]
        MVG = [SM[:, 112 + 8 * i:120 + 8 * i].rearrange("p (t m) -> p t m", m=2) for i in range(2)]
        VEG, RSG, NMG = ([SM[:, at + 4 * i:at + 4 + 4 * i] for i in range(2)] for at in (128, 136, 144))

        pe, dve, act, pool = (Queue(sem(n)) for n in ("s_pe", "s_dve", "s_act", "s_pool"))
        sp = Queue(sem("s_sp"))

        def counter(name):
            return [sem(name), 0]

        c_ring = [counter(f"c_ring{i}") for i in range(4)]
        c_x = [counter(f"c_x{i}") for i in range(9)]
        c_x2 = [counter(f"c_x2{i}") for i in range(2)]
        c_fl = [counter(f"c_fl{i}") for i in range(NF)]
        c_fs = [counter(f"c_fs{i}") for i in range(NF)]
        c_wst = [counter(f"c_wst{i}") for i in range(2)]
        c_b1, c_b2, c_bias, c_gb, c_gw = (counter(n) for n in ("c_b1", "c_b2", "c_bias", "c_gb", "c_gw"))

        free = [None] * 8

        def mm(o, l, r, start, stop):
            return lambda e: nc.tensor.matmul(o, l, r, start=start, stop=stop, skip_group_check=True)

        def tr(o, i, n=128):
            return lambda e: nc.tensor.transpose(o, i, IDN[0:n, 0:n])

        def copy_act(o, i):
            return lambda e: nc.scalar.copy(o, i)

        def tt(o, p, q, op):
            return lambda e: nc.vector.tensor_tensor(o, p, q, op)

        def const(o, v):
            return pool(lambda e: nc.gpsimd.memset(o, v), (pool.sem, pool.count))

        const(IDN, 0.0)
        const(TRI, 1.0)
        const(MBD, 0.0)
        const(SEL, 0.0)
        const(NHALF, -0.5)
        const(MG[:, :, 256:280], 0.0)

        def select(t, pattern, cm, base, op, fill):
            return pool(lambda e: nc.gpsimd.affine_select(out=t, in_=t, compare_op=op, fill=fill, base=base,
                                                          pattern=pattern, channel_multiplier=cm),
                        (pool.sem, pool.count))

        t_idn = select(IDN, [[-1, 128]], 1, 0, ALU.not_equal, 1.0)
        select(TRI, [[1, 128]], -1, 0, ALU.is_ge, 0.0)
        for r in range(4):
            t_cst = pool(lambda e, r=r: nc.gpsimd.memset(MBD[32 * r:32 * r + 32, 32 * r:32 * r + 32], 1.0),
                         (pool.sem, pool.count))
        for j in range(4):
            t_cst = select(SEL[:, 0:287], [[-1, 287]], 32, 31 - 1024 * j, ALU.not_equal, 1.0)

        t_tri = act(copy_act(UPTO, TRI), t_cst)
        t_tri = act(lambda e: nc.scalar.activation(AFTER, TRI, ACT.Identity, scale=-1.0, bias=1.0), t_cst)

        ring_tok, ring_free = {}, [None] * 4

        def load_chunk(g, *waits):
            e, part = (g // 4) % E, g % 4
            slot = g % 4
            if part < 2:
                src = w1[e, 0:512, :].rearrange("(p k) n -> p k n", k=4)[:, 2 * part:2 * part + 2, :]
                dst = ring[slot].rearrange("p (k n) -> p k n", k=2)
            else:
                src = w2[e, 0:2048, :].rearrange("(j c i) n -> c j (i n)", j=4, i=4)[:, 2 * part - 4:2 * part - 2, :]
                dst = ring[slot].rearrange("p (j n) -> p j n", j=2)
            ring_tok[g] = sp.dma(c_ring[slot], dst, src, ring_free[slot], *waits)

        ln_n, mv_free = [0], [None] * 4

        def stats(src, src_tok):
            i = ln_n[0] % 4
            ln_n[0] += 1
            t = dve(lambda e: nc.vector.bn_stats(ST6[i], src), src_tok)
            t = dve(lambda e: nc.vector.bn_aggr(MV[i], ST6[i]), t, mv_free[i])
            t = dve(lambda e: nc.vector.tensor_scalar(VE[i], MV[i][:, 1:2], EPS, None, ALU.add), t)
            return i, pool(lambda e: nc.gpsimd.tensor_tensor(RS[i], VE[i], NHALF, ALU.pow), t)

        def apply(stat, src, dst, *waits):
            i, t = stat
            mv_free[i] = dve(lambda e: nc.vector.tensor_scalar(dst, src, MV[i][:, 0:1], RS[i], ALU.subtract, ALU.mult),
                           t, *waits)
            return mv_free[i]

        order = list(range(8))

        def bank(among=range(8)):
            k = next(k for k in order if k in among)
            order.remove(k)
            order.append(k)
            return k

        ANY, NOT_S = (0, 1, 4, 5, 6, 7), (0, 1)
        banks, tbanks = [range(8)], [range(8)]

        xt3_free = [None, None]
        logit_tok = {}
        mt_free = [None]
        l_free = [None] * 4
        xt3_tok = {}

        def gate_transpose(n, src, tok):
            k = bank(tbanks[0])
            for j in range(4):
                t = pe(tr(ps[:, k, 128 * j:128 * j + 128], src[:, 128 * j:128 * j + 128]),
                       tok, free[k], t_idn, inc=j == 3)
            i = n % 2
            free[k] = xt3_tok[n] = act(copy_act(XT3[i], ps[:, k, :].rearrange("p (k t) -> p k t", k=4)),
                                       t, xt3_free[i])

        def gate_logits(n):
            b, c, i = n // 8, n % 8, n % 2
            q = 32 * (b % 4)
            k = bank(banks[0])
            for j in range(4):
                t = pe(mm(ps[q:q + 32, k, 0:128], GT[:, j, :], XT3[i][:, j, :], j == 0, j == 3),
                       xt3_tok[n], free[k], t_gt, inc=j == 3)
            xt3_free[i] = t
            free[k] = logit_tok[n] = act(
                lambda e: nc.scalar.activation(L[q:q + 32, 128 * c:128 * c + 128], ps[q:q + 32, k, 0:128],
                                               ACT.Identity, bias=GB[q:q + 32, :]), t, t_gb, l_free[b % 4])

        def topk(b, m):
            q = 32 * (b % 4)
            R_ = slice(q, q + 32)
            W = M[m][R_, b // 4, :]
            t = dve(lambda e: nc.vector.max(T8[R_, :], L[R_, :]), logit_tok[8 * b + 7])
            t2 = dve(lambda e: nc.vector.match_replace(W, T8[R_, :], L[R_, :], LOWEST), t)
            t = dve(lambda e: nc.vector.tensor_scalar(NMX[R_, :], T8[R_, 0:1], -1.0, None, ALU.mult), t)
            t2 = dve(tt(W, L[R_, :], W, ALU.not_equal), t2)
            return act(lambda e: nc.scalar.activation(L[R_, :], L[R_, :], ACT.Exp, bias=NMX[R_, :],
                                                      accum_out=SUM[R_, :]), t, t2), t2

        def weights(b, m, toks):
            q = 32 * (b % 4)
            R_ = slice(q, q + 32)
            W = M[m][R_, b // 4, :]
            t = dve(lambda e: nc.vector.reciprocal(RSUM[R_, :], SUM[R_, :]), toks[0])
            l_free[b % 4] = t = dve(lambda e: nc.vector.scalar_tensor_tensor(
                out=W, in0=L[R_, :], scalar=RSUM[R_, :], in1=W, op0=ALU.mult, op1=ALU.mult), t, toks[1])
            return t

        def merge_transpose(b, m, tok):
            q = 32 * (b % 4)
            k = bank(banks[0])
            for c in range(8):
                t = pe(lambda e, c=c: nc.tensor.transpose(ps[:, k, 32 * c:32 * c + 32],
                                                          M[m][q:q + 32, b // 4, 128 * c:128 * c + 128],
                                                          IDN[q:q + 32, q:q + 32]), tok, free[k], inc=c == 7)
            free[k] = t = act(copy_act(MT, ps[:, k, 0:256].rearrange("p (c e) -> p c e", c=8)), t, mt_free[0])
            return t

        def merge_tokens(b, m, tok, xn_tok):
            k = bank(banks[0])
            for h in range(2):
                for c in range(4):
                    t = pe(mm(ps[32 * c:32 * c + 32, k, :], MT[:, 4 * h + c, :], TILES[m][(8 * b + 4 * h + c) % len(TILES[m])],
                              h == 0, h == 1), tok, xn_tok, free[k], inc=h == 1 and c == 3)
            mt_free[0] = merged[b + 8 * m] = t
            free[k] = t = act(copy_act(PR3, ps[:, k, :]), t, pr3_free[0])
            return t

        def merge_end(b, tok):
            k = bank(banks[0])
            for j in range(4):
                t = pe(tr(ps[:, k, 128 * j:128 * j + 128], PR3.rearrange("p (c k) -> p k c", k=4)[:, j, :]),
                       tok, free[k], inc=j == 3)
            pr3_free[0] = t
            free[k] = mg_tok[b] = dve(lambda e: nc.vector.tensor_reduce(
                MG[:, :, 0:256].rearrange("p k (e b) -> p k e b", b=8)[:, :, :, b],
                ps[:, k, :].rearrange("p (k q e) -> p k e q", k=4, q=4), AX.X, ALU.add), t, mg_free[0])

        pend = {}

        def gate(b, m, step):
            if step == 0:
                pend[b] = topk(b, m)
            elif step == 1:
                pend[b] = weights(b, m, pend[b])
            elif step == 2:
                pend[b] = merge_transpose(b, m, pend[b])
            elif step == 3:
                pend[b] = merge_tokens(b, m, pend[b], xn_tok[8 * b + 7])
            elif step == 4:
                merge_end(b, pend[b])

        merged = {}
        pr3_free = [None]
        mg_tok, mg_free = {}, [None]

        t_gw = sp.dma(c_gw, GW, gate_w)
        for r in range(4):
            t_gb = sp.dma(c_gb, GB[32 * r:32 * r + 32, :], gate_b.rearrange("(e a) -> e a", a=1))
        xl_tok, xl_free = {}, [None] * 4

        def load_x(g, *waits):
            xl_tok[g] = sp.dma(c_x[g % NX4], XLA[g % NX4], xs[4 * g:4 * g + 4].rearrange("t p d -> p t d"), *waits)

        for g in range(7):
            load_x(g)
        k = bank()
        for j in range(4):
            t = pe(lambda e, j=j, k=k: nc.tensor.transpose(ps[:, k, 32 * j:32 * j + 32], GW[:, 128 * j:128 * j + 128],
                                                      IDN[0:32, 0:32]), t_gw, t_idn, inc=j == 3)
        free[k] = t_gt = act(copy_act(GT, ps[:, k, 0:128].rearrange("p (k e) -> p k e", k=4)), t)

        for g in range(7, NX4):
            load_x(g, t_gt)

        xn_tok, stat = {}, {}
        NG = NT // 4
        rs_tok, nm_tok, norm_tok, xt4_tok, xt4_free = {}, {}, {}, {}, [None] * 2
        def stats4(g):
            i = g % 2
            ts = []
            for j in range(4):
                ts.append(dve(lambda e, j=j: nc.vector.bn_stats(ST6[j], XLA[g % NX4][:, j, :]), xl_tok[g]))
            for j in range(4):
                t = dve(lambda e, j=j: nc.vector.bn_aggr(MVG[i][:, j, :], ST6[j]), ts[j])
            t = dve(lambda e: nc.vector.tensor_scalar(VEG[i], MVG[i][:, :, 1], EPS, None, ALU.add), t)
            rs_tok[g] = pool(lambda e: nc.gpsimd.tensor_tensor(RSG[i], VEG[i], NHALF.broadcast_to([128, 4]), ALU.pow),
                             t, nm_tok.get(g - 2), norm_tok.get(g - 2))

        def norm_mean(g):
            i = g % 2
            nm_tok[g] = dve(lambda e: nc.vector.scalar_tensor_tensor(
                out=NMG[i], in0=MVG[i][:, :, 0], scalar=-1.0, in1=RSG[i], op0=ALU.mult, op1=ALU.mult), rs_tok[g],
                norm_tok.get(g - 2))

        def norm(g, j):
            i = g % 2
            norm_tok[g] = xn_tok[4 * g + j] = act(lambda e: nc.scalar.activation(
                XLA[g % NX4][:, j, :], XLA[g % NX4][:, j, :], ACT.Identity, bias=NMG[i][:, j:j + 1],
                scale=RSG[i][:, j:j + 1]), nm_tok[g])

        def transposed(g, j):
            i, n = g % 2, 4 * g + j
            k = bank()
            for m in range(4):
                t = pe(tr(ps[:, k, 128 * m:128 * m + 128], XLA[g % NX4][:, j, 128 * m:128 * m + 128]),
                       xn_tok[n], free[k], t_idn, inc=m == 3)
            dst = XT4[i][:, :, 128 * j:128 * j + 128]
            src = ps[:, k, :].rearrange("p (k t) -> p k t", k=4)
            if j == 3 or (j == 1 and g % 2 == 0):
                free[k] = xt4_tok[n] = dve(lambda e: nc.vector.tensor_copy(dst, src), t, xt4_free[i])
            else:
                free[k] = xt4_tok[n] = act(copy_act(dst, src), t, xt4_free[i])

        def logits4(g):
            b, i = g // 2, g % 2
            q = 32 * (b % 4)
            k = bank()
            for j in range(4):
                t = pe(mm(ps[q:q + 32, k, :], GT[:, j, :], XT4[i][:, j, :], j == 0, j == 3),
                       xt4_tok[4 * g + 2], xt4_tok[4 * g + 3], free[k], t_gt, inc=j == 3)
            xt4_free[i] = t
            free[k] = logit_tok[4 * g + 3] = act(
                lambda e: nc.scalar.activation(L[q:q + 32, 512 * i:512 * i + 512], ps[q:q + 32, k, :],
                                               ACT.Identity, bias=GB[q:q + 32, :]), t, t_gb, l_free[b % 4])

        def batch(g, after):
            b = (g - after) // 2
            return [b] if (g - after) % 2 == 0 and 0 <= b < B else []

        for g in range(-2, NG + 5):
            if 0 <= g + 1 < NG:
                norm_mean(g + 1)
            if g + 2 < NG:
                stats4(g + 2)
            for b in batch(g, 4):
                pend[b] = weights(b, 0, pend[b])
            for b in batch(g, 6):
                merge_end(b, pend[b])
            for j in range(4):
                if 0 <= g < NG:
                    transposed(g, j)
                if 0 <= g + 1 < NG:
                    norm(g + 1, j)
            if 0 <= g - 1 < NG:
                logits4(g - 1)
            for b in batch(g, 4):
                pend[b] = merge_transpose(b, 0, pend[b])
            for b in batch(g, 5):
                pend[b] = merge_tokens(b, 0, pend[b], xn_tok[8 * b + 7])
                for n in (2 * b + NX4, 2 * b + 1 + NX4):
                    if n < NG:
                        load_x(n, merged[b])
            for b in batch(g, 3):
                pend[b] = topk(b, 0)
            if g in (7, 9, 11, 13):
                load_chunk((g - 7) // 2)
        t_obd0 = pool(lambda e: nc.gpsimd.memset(big[:, obd_at:obd_at + 4096], 0.0), xt4_free[0], xt4_free[1])

        def experts(first, extra):
            hb, tb, pb = {}, {}, {}
            h_tok, hg_tok, ht_tok, pt_tok, hgf, htf, ptf = {}, {}, {}, {}, [None] * 2, [None] * 2, [None] * 2
            o_last = None
            for e in range(E + 1):
                if e < E:
                    g = first + 4 * e
                    i = e % 2
                    k = i
                    for j in range(4):
                        r = 32 * j + e
                        pe(mm(ps[32 * j:32 * j + 32, k, :], IDN[:, r:r + 1].broadcast_to([128, 32]), B1,
                              True, False), free[k], t_b1, mg_tok[7], inc=False)
                    for kt in range(4):
                        v = ring[(g + kt // 2) % 4].rearrange("p (k n) -> p k n", k=2)
                        for j in range(4):
                            t = pe(mm(ps[32 * j:32 * j + 32, k, :], MG[:, kt, 8 * e:8 * e + 32],
                                      v[:, kt % 2, 512 * j:512 * j + 512], False, kt == 3),
                                   ring_tok[g + kt // 2], inc=kt % 2 == 1 and j == 3)
                        if kt % 2 == 1:
                            slot = (g + kt // 2) % 4
                            ring_free[slot] = t
                            if g + kt // 2 + 4 < first + 128:
                                load_chunk(g + kt // 2 + 4)
                    mg_free[0] = t
                    free[k] = t = act(lambda q, i=i, k=k: nc.scalar.activation(HG[i], ps[:, k, :], ACT.Gelu),
                                      t, hgf[i])
                    hg_tok[e] = t
                if e >= 1:
                    p = e - 1
                    i = p % 2
                    for half in range(2):
                        off = 128 * half + 31 - p
                        t = pe(mm(ps[:, 6 + half, :], SEL[:, off:off + 128], PT[i], p == 0, p == E - 1),
                               pt_tok[p], free[6 + half], t_cst)
                    ptf[i] = o_last = t
                if e < E:
                    i = e % 2
                    k = 2 + i
                    for q in range(4):
                        t = pe(tr(ps[:, k, 128 * q:128 * q + 128],
                                  HG[i].rearrange("p (c t) -> p t c", t=4)[:, q, :]),
                               hg_tok[e], free[k], inc=q == 3)
                    hgf[i] = t
                    free[k] = t = dve(lambda q, i=i, k=k: nc.vector.tensor_copy(HT[i], ps[:, k, :]), t, htf[i])
                    k = 4 + i
                    for j in range(4):
                        v = ring[(g + 2 + j // 2) % 4].rearrange("p (j i n) -> p j i n", j=2, i=4)
                        for q in range(4):
                            t2 = pe(mm(ps[32 * q:32 * q + 32, k, :], HT[i][:, 128 * q + 32 * j:128 * q + 32 * j + 32],
                                       v[:, j % 2, q, :], j == 0, j == 3),
                                    t, free[k], ring_tok[g + 2 + j // 2], inc=j % 2 == 1 and q == 3)
                        if j % 2 == 1:
                            slot = (g + 2 + j // 2) % 4
                            ring_free[slot] = t2
                            if g + 2 + j // 2 + 4 < first + 128:
                                load_chunk(g + 2 + j // 2 + 4)
                    htf[i] = t2
                    free[k] = pt_tok[e] = act(copy_act(PT[i], ps[:, k, :]), t2, ptf[i])
                    extra(e)
            toks = []
            for b in range(B):
                q = 32 * (b % 4)
                R = slice(q, q + 32)
                toks.append(dve(tt(OBD[R, b, :], ps[R, 6 + b // 4, :], B2[R, :], ALU.add), o_last, t_b2, t_obd0,
                                obd_free[0]))
            free[6] = free[7] = toks[-1]
            return toks

        obd_free = [None]
        for j in range(4):
            t_b1 = sp.dma(c_b1, B1[32 * j:32 * j + 32, :], w1[:, 512, 512 * j:512 * j + 512])
            t_b2 = sp.dma(c_b2, B2[32 * j:32 * j + 32, :], w2[:, 2048, :])
        for t_, s_ in ((BQ, bq), (BK, bk), (BV, bv), (BO, bo)):
            t_bias = sp.dma(c_bias, t_, s_.partition_broadcast(128))

        wl_tok, wls_free = [None], [None] * 2
        c_wls = [counter(f"c_wls{i}") for i in range(2)]
        c_wl = counter("c_wl")
        wst_free = [t_gt, None]
        wst_tok = {}

        def prepare(e):
            if e % 6 == 0 and e < 24:
                m = e // 6
                wst_tok[m] = act.dma(c_wst[m % 2], WST[m % 2],
                                     (Wq, Wk, Wv, Wo)[m].rearrange("(o p) i -> p o i", p=128), wst_free[m % 2])
            m, kt = e // 6, e % 6 - 1
            if 0 <= kt < 4 and m < 4:
                k = 6 - 6 + 2 + (e + 1) % 2
                for o in range(4):
                    t = pe(tr(ps[:, k, 128 * o:128 * o + 128], WST[m % 2][:, o, 128 * kt:128 * kt + 128]),
                           wst_tok[m], free[k], inc=o == 3)
                wst_free[m % 2] = t
                t = act(copy_act(WTH[m][:, kt, :], ps[:, k, :]), t, xl_free[3])
                i = (4 * m + kt) % 2
                free[k] = t = dve(tt(WLS[i], ps[:, k, :], WTH[m][:, kt, :].bitcast(F), ALU.subtract), t, wls_free[i])
                wl_tok[0] = wls_free[i] = act.dma(c_wls[i], wl[m, kt], WLS[i].bitcast(F), t)

        o_tok = experts(0, prepare)
        for m in range(4):
            t_w = sp.dma(c_wl, WTL[m].bitcast(F), wl[m].rearrange("k p n -> p k n"),
                         wls_free[0], wls_free[1], ring_free[0], ring_free[1])

        fl_tok, fs_tok = {}, {}

        def load_f(n, *waits, on=sp):
            fl_tok[n] = on.dma(c_fl[n % NF], FX[n % NF], x2s[n], fs_tok.get(n - NF), x2_tok[NT - 1], *waits)

        x1_tok, x1b_tok, x2_tok, xnt_tok, xt_tok = {}, {}, {}, {}, {}
        q_tok, k_tok, v_tok = {}, {}, {}
        x1_free, x2_free, xnf, xtf = [None] * 3, [None] * 2, [None], [None] * 2
        xl_free = [None] * 2
        kf, vf = [[], []], [[], []]
        once = {n_: None for n_ in ("KT", "QH", "QT", "QB", "AT", "KV", "TMP", "KH", "ST")}
        kv_tok = pr_tok = None
        z_qb = pool(lambda e: nc.gpsimd.memset(QB, 0.0), wst_free[0], wst_free[1])
        def residual(n):
            b, c = n // 8, n % 8
            k = bank(ANY)
            t = pe(mm(ps[:, k, :], M[0][:, b // 4, 128 * c:128 * c + 128], OBD[:, b, :], True, True),
                   free[k], o_tok[b], o_tok[7])
            obd_free[0] = t
            i, j = n % 3, n % 2
            free[k] = xl_free[j] = x1_tok[n] = dve(
                lambda e: nc.vector.scalar_tensor_tensor(out=X1[i], in0=ps[:, k, :], scalar=0.5, in1=XL[j],
                                                         op0=ALU.mult, op1=ALU.add),
                t, xl_tok[NT + n], x1_free[i], ring_free[2], ring_free[3])
            stat[n] = stats(X1[i], x1_tok[n])

        def x_apply(n):
            i = n % 3
            xnt_tok[n] = apply(stat[n], X1[i], XN, xnf[0])
            x1b_tok[n] = pool(lambda e: nc.gpsimd.tensor_tensor(X1[i], X1[i], BO, ALU.add), xnt_tok[n], t_bias)

        def load_x1(n):
            i = n % 2
            xl_tok[NT + n] = sp.dma(c_x[i], XL[i], xs[n], xl_free[i])

        def x_transpose(n):
            k, i = bank(NOT_S), n % 2
            for j in range(4):
                t = pe(tr(ps[:, k, 128 * j:128 * j + 128], XN[:, 128 * j:128 * j + 128]),
                       xnt_tok[n], free[k], inc=j == 3)
            xnf[0] = t
            v = ps[:, k, :].rearrange("p (k t) -> p k t", k=4)
            t = act(copy_act(XTH[i], v), t, xtf[i])
            free[k] = xt_tok[n] = dve(tt(XTL[i], v, XTH[i].bitcast(F), ALU.subtract), t)

        def project(n, w, dst, bias, exp, waits):
            k, i = bank(NOT_S if w == 2 else ANY), n % 2
            for j in range(4):
                pe(mm(ps[:, k, :], XTH[i][:, j, :], WTH[w][:, j, :], j == 0, False), xt_tok[n], free[k], t_w, inc=False)
                pe(mm(ps[:, k, :], XTH[i][:, j, :], WTL[w][:, j, :], False, False), inc=False)
                t = pe(mm(ps[:, k, :], XTL[i][:, j, :], WTH[w][:, j, :], False, j == 3), inc=j == 3)
            if w == 2:
                xtf[i] = t
            free[k] = t = dve(tt(dst, ps[:, k, :], bias, ALU.add), t, t_bias, *waits)
            if exp:
                t = act(lambda e: nc.scalar.activation(dst, dst, ACT.Exp), t)
            return t

        def h4(t):
            return t.rearrange("p (g n) -> p g n", g=4)

        for n in range(2):
            load_x1(n)
        banks[0], tbanks[0] = ANY, NOT_S
        for n in range(-3, NT + 6):
            live = 0 <= n < NT
            nxt = 0 <= n + 1 < NT
            if live:
                b, c, i = n // 8, n % 8, n % 2
                if c < 7:
                    pe(mm(ps[:, 2, :], AFTER, KH, False, False), pr_tok, inc=False)
                    once["KH"] = pe(mm(ps[:, 2, :], AFTER, KL, False, False))
            if 0 <= n + 2 < NT:
                residual(n + 2)
                if n + 4 < NT:
                    load_x1(n + 4)
            if live:
                k = bank(ANY)
                for g in range(4):
                    t = pe(tr(ps[:, k, 128 * g:128 * g + 128], Ks[i][:, 128 * g:128 * g + 128]), free[k], k_tok[n],
                           inc=g == 3)
                free[k] = kt_tok = act(copy_act(KT, ps[:, k, :]), t, once["KT"])
                k = bank(ANY)
                for g in range(4):
                    t = pe(tr(ps[:, k, 128 * g:128 * g + 128], QH[:, 128 * g:128 * g + 128]), free[k], qh_tok,
                           inc=g == 3)
                once["QH"] = t
                for r in range(4):
                    R_ = slice(32 * r, 32 * r + 32)
                    tq = act(copy_act(QB[R_, :, r, :], ps[R_, k, :].rearrange("p (g t) -> p g t", g=4)),
                             t, once["QB"], z_qb)
                free[k] = qt_tok = act(copy_act(QT, ps[:, k, :]), t, once["QT"])
            if nxt:
                q_tok[n + 1] = project(n + 1, 0, Qs[(n + 1) % 2], BQ, True, [])
            if 0 <= n + 2 < NT:
                x_apply(n + 2)
            if n >= 1 and n - 1 < NT:
                xn_tok[n - 1] = apply(x2_stat, X2, XN3[(n - 1) % NX], merged.get(8 + (n - 1 - NX) // 8 if n > NX else None))
                x2_free[1] = xn_tok[n - 1]
            if nxt:
                j = (n + 1) % 2
                k_tok[n + 1] = project(n + 1, 1, Ks[j], BK, True, kf[j])
                t = act(copy_act(KH, Ks[j]), k_tok[n + 1], once["KH"])
                kh_tok = pool(lambda e, j=j: nc.gpsimd.tensor_tensor(KL, Ks[j], KH.bitcast(F), ALU.subtract),
                              t, once["KH"])
                kf[j] = [kh_tok]
            if 0 <= n + 2 < NT:
                x_transpose(n + 2)
            if 1 <= n <= NT:
                gate_transpose(n - 1, XN3[(n - 1) % NX], xn_tok[n - 1])
            if live:
                s_tok = []
                for g in range(4):
                    s_tok.append(pe(mm(ps[:, 4 + g, :], h4(KT)[:, g, :], QB[:, g, :, :], True, True),
                                    free[4 + g], kt_tok, tq))
                once["KT"] = once["QB"] = s_tok[3]
                for g in range(4):
                    free[4 + g] = st_tok = dve(tt(h4(ST[:, g, :]), h4(ps[:, 4 + g, :]),
                                                  TRI.unsqueeze(1).broadcast_to([128, 4, 128]), ALU.mult),
                                               s_tok[g], once["ST"])
            if nxt:
                v_tok[n + 1] = project(n + 1, 2, Vs[(n + 1) % 2], BV, False, vf[(n + 1) % 2])
            if live:
                for g in range(4):
                    if c:
                        ti = pe(mm(ps[:, 3, 128 * g:128 * g + 128], h4(KV)[:, g, :], h4(QT)[:, g, :], True, False),
                                free[3], kv_tok, qt_tok, inc=g == 3)
                    for r in range(4):
                        o = ps[32 * r:32 * r + 32, 3, 128 * g:128 * g + 128]
                        t = pe(mm(o, Vs[i][:, 128 * g + 32 * r:128 * g + 32 * r + 32],
                                  ST[:, g, 128 * r:128 * r + 128], c == 0, True), free[3], st_tok, v_tok[n],
                               inc=g == 3 and r == 3)
                once["ST"] = once["QT"] = t
                if c:
                    once["KV"] = ti
                t = act(copy_act(ATH, ps[:, 3, :]), t, once["AT"])
                free[3] = at_tok = dve(tt(ATL, ps[:, 3, :], ATH.bitcast(F), ALU.subtract), t)
            if nxt:
                j, first = (n + 1) % 2, (n + 1) % 8 == 0
                pe(mm(ps[:, 2, :], UPTO, KH, first, False), kh_tok, t_tri, pr_tok, inc=False)
                once["KH"] = t = pe(mm(ps[:, 2, :], UPTO, KL, False, False))
                pr_tok = t = dve(tt(PR, ps[:, 2, :], Qs[j], ALU.mult), t, q_tok[n + 1])
                t = dve(lambda e: nc.vector.tensor_reduce(DEN, PR.rearrange("p (h d) -> p h d", h=16),
                                                          AX.X, ALU.add), t)
                t = dve(lambda e: nc.vector.reciprocal(RDEN, DEN), t)
                qh_tok = dve(tt(QH.rearrange("p (h d) -> p h d", h=16), Qs[j].rearrange("p (h d) -> p h d", h=16),
                                RDEN.unsqueeze(2).broadcast_to([128, 16, 32]), ALU.mult), t, once["QH"])
            if live and c < 7:
                k = bank(ANY)
                for g in range(4):
                    t = pe(mm(ps[:, k, 128 * g:128 * g + 128], Ks[i][:, 128 * g:128 * g + 128],
                              Vs[i][:, 128 * g:128 * g + 128], True, True), free[k], inc=g == 3)
                dst = KV if c == 0 else TMP
                free[k] = kv_tok = dve(tt(h4(dst), h4(ps[:, k, :]), MBD.unsqueeze(1).broadcast_to([128, 4, 128]),
                                          ALU.mult), t, once["KV"], once["TMP"])
                if c:
                    kv_tok = once["TMP"] = pool(lambda e: nc.gpsimd.tensor_tensor(KV, KV, TMP, ALU.add), kv_tok)
            if live:
                t = (pe.sem, pe.count)
                kf[i] = kf[i] + [t]
                vf[i] = [t]
            if live:
                k = bank(ANY)
                for g in range(4):
                    pe(mm(ps[:, k, :], h4(ATH)[:, g, :], WTH[3][:, g, :], g == 0, False), free[k], at_tok, inc=False)
                    pe(mm(ps[:, k, :], h4(ATH)[:, g, :], WTL[3][:, g, :], False, False), inc=False)
                    t = pe(mm(ps[:, k, :], h4(ATL)[:, g, :], WTH[3][:, g, :], False, g == 3), inc=g == 3)
                once["AT"] = t
                j = n % 3
                free[k] = x1_free[j] = t = dve(tt(X2, ps[:, k, :], X1[j], ALU.add), t, x1b_tok[n], x2_free[0], x2_free[1])
                x2_free[0] = x2_tok[n] = sp.dma(c_x2[i], x2s[n], X2, t)
                x2_stat = stats(X2, t)
            if 1 <= n <= NT:
                gate_logits(n - 1)
            if n >= 9:
                gate((n - 9) // 8, 1, (n - 9) % 8)
            if n == NT - 2:
                load_chunk(128, (pe.sem, pe.count))
            if n == NT:
                att = [(pe.sem, pe.count), (dve.sem, dve.count), (pool.sem, pool.count), (act.sem, act.count)]
                for g in range(129, 132):
                    load_chunk(g, x2_free[0], *att)
                for m in range(NF):
                    load_f(m, *att)

        o_tok = experts(128, lambda e: None)
        for n in range(NT):
            b, c, i = n // 8, n % 8, n % NF
            k = n % 6
            t = pe(mm(ps[:, k, :], M[1][:, b // 4, 128 * c:128 * c + 128], OBD[:, b, :], True, True),
                   free[k], o_tok[b], o_tok[7])
            free[k] = t = dve(lambda e, i=i, k=k: nc.vector.scalar_tensor_tensor(
                out=FX[i], in0=ps[:, k, :], scalar=0.5, in1=FX[i], op0=ALU.mult, op1=ALU.add), t, fl_tok[n])
            fs_tok[n] = sp.dma(c_fs[i], outs[n], FX[i], t)
            if n >= 4 and n - 4 + NF < NT:
                load_f(n - 4 + NF, on=act)
        sp.wait(*[fs_tok[n] for n in range(NT - NF, NT)])

        block = ctx.enter_context(nc.Block())

        @block.sync
        def _(eng):
            sp.issue(eng)

        @block.gpsimd
        def _(eng):
            pool.issue(eng)

        @block.scalar
        def _(eng):
            act.issue(eng)

        @block.vector
        def _(eng):
            dve.issue(eng)

        @block.tensor
        def _(eng):
            pe.issue(eng)


_INS = ["x", "Wq", "bq", "Wk", "bk", "Wv", "bv", "Wo", "bo"]
_FFN = ["gate_w", "gate_b", "w1", "w2"]


def kernel(**inputs):
    import numpy as _np
    import concourse.bacc as _bacc
    from concourse import mybir as _mybir
    from concourse.bass_utils import run_bass_kernel_spmd as _run

    nc = _bacc.Bacc("TRN2", target_bir_lowering=False, num_devices=1, dynamic_dma_scratch_size=1024)
    arrays, args = {}, []
    for name in ["L0_attn_" + n for n in _INS] + ["L0_ffn_" + n for n in _FFN]:
        a = _np.ascontiguousarray(inputs[name])
        arrays[f"in_{name}"] = a
        args.append(nc.dram_tensor(f"in_{name}", a.shape, _mybir.dt.from_np(a.dtype), kind="ExternalInput").ap())
    out = nc.dram_tensor("out_x", (8, 1024, 512), _mybir.dt.float32, kind="ExternalOutput").ap()
    macaron_block(nc, *args, out)
    r = _run(nc, [arrays], core_ids=[0])
    return r.results[0]["out_x"]
```

```python
import concourse.bass as bass
from concourse import mybir
from contextlib import ExitStack


class Queue:

    def __init__(self, sem):
        self.sem, self.count, self.items = sem, 0, []

    def __call__(self, fn, *waits, inc=True):
        if inc:
            self.count += 1
        self.items.append((waits, fn, (self.sem, 1) if inc else None))
        return (self.sem, self.count)

    def dma(self, counter, out, in_, *waits):
        counter[1] += 16
        self.items.append((waits, lambda e: e.dma_start(out, in_), (counter[0], 16)))
        return (counter[0], counter[1])

    def wait(self, *waits):
        self.items.append((waits, None, None))

    def issue(self, eng):
        seen = {}
        for waits, fn, inc in self.items:
            for w in waits:
                if w is not None and seen.get(id(w[0]), 0) < w[1]:
                    eng.wait_ge(w[0], w[1])
                    seen[id(w[0])] = w[1]
            if fn is not None:
                ins = fn(eng)
                if inc is not None:
                    ins.then_inc(inc[0], inc[1])


def macaron_block(nc, x, Wq, bq, Wk, bk, Wv, bv, Wo, bo, gate_w, gate_b, w1, w2, out):
    F = mybir.dt.float32
    R = mybir.dt.float32r
    ALU = mybir.AluOpType
    ACT = mybir.ActivationFunctionType
    AX = mybir.AxisListType

    B, S, D, E, H = 8, 1024, 512, 32, 2048
    NT = B * S // 128
    LOWEST = -3.4028234663852886e38
    EPS = 1e-5

    wl = nc.dram_tensor("wl_scratch", (4, 4, 128, D), F).ap()
    x2d = nc.dram_tensor("x2_scratch", (B, S, D), F).ap()
    xs = x.rearrange("b (c p) d -> (b c) p d", p=128)
    x2s = x2d.rearrange("b (c p) d -> (b c) p d", p=128)
    outs = out.rearrange("b (c p) d -> (b c) p d", p=128)

    ctx = ExitStack()
    with ctx:
        SIZE = 57040
        CUT = 38272
        big = ctx.enter_context(nc.sbuf_tensor("big", [128, CUT], F))
        big2 = ctx.enter_context(nc.sbuf_tensor("big2", [128, SIZE - CUT], F))
        base = nc.sbuf_base - 4 * SIZE
        ps = ctx.enter_context(nc.psum_tensor("ps", [128, 8, 512], F))

        def sem(name):
            return ctx.enter_context(nc.semaphore(name))

        class Area:
            def __init__(self, at):
                self.at = at

            def take(self, n):
                self.at += n
                assert self.at <= CUT or self.at - n >= CUT
                return big[:, self.at - n:self.at] if self.at <= CUT else big2[:, self.at - n - CUT:self.at - CUT]

        a = Area(0)
        ring = [a.take(4096) for _ in range(4)]
        wth_at = a.at
        a.take(8192)
        m_at = a.at
        M = [a.take(2048).rearrange("p (h t) -> p h t", h=2) for _ in range(2)]
        obd_at = a.at
        OBD = a.take(4096).rearrange("p (b n) -> p b n", b=8)
        MG = a.take(1120).rearrange("p (k c) -> p k c", k=4)
        b_at = a.at
        B1, B2 = a.take(512), a.take(512)
        IDN, TRI, MBD = (a.take(128) for _ in range(3))
        tri_at = a.at
        a.take(256)
        SEL = a.take(288)
        GT = a.take(128).rearrange("p (k e) -> p k e", k=4)
        BQ, BK, BV, BO = (a.take(512) for _ in range(4))
        SM = a.take(256)
        xn3_at = a.at
        NX = 12
        XN3 = [a.take(512) for _ in range(NX)]
        XT3 = [a.take(512).rearrange("p (k t) -> p k t", k=4) for _ in range(2)]
        L = a.take(1024)
        MT = a.take(256).rearrange("p (c e) -> p c e", c=8)
        PR3 = a.take(512)
        qb_at = a.at
        a.take(2048)
        ST = a.take(2048).rearrange("p (g n) -> p g n", g=4)
        qbl_at = a.at
        a.take(2048)
        ring += [big2[:, qbl_at - CUT:qbl_at - CUT + 4096], big[:, wth_at:wth_at + 4096],
                 big[:, wth_at + 4096:wth_at + 8192], big[:, obd_at:obd_at + 4096]]
        QT, KV, TMP = (a.take(512) for _ in range(3))
        PR = TMP
        kh_at = a.at
        a.take(1024)
        ath_at = a.at
        a.take(1024)
        assert a.at <= SIZE

        assert xn3_at == CUT

        s = Area(8192)
        X1 = [s.take(512) for _ in range(4)]
        X2, XN = s.take(512), s.take(512)
        xt_at = s.at
        s.take(2048)
        Qs = [s.take(512) for _ in range(2)]
        k_at = s.at
        s.take(1024)
        Vs = [s.take(512) for _ in range(2)]
        assert s.at == 16384

        def halves(name, at, n, dt=R):
            return nc.alloc_sbuf_tensor_at(name, [128, n], dt, offset=base + 4 * at)

        WTH = [halves(f"wth{m}", wth_at + 2048 * m, 2048)[:, :].rearrange("p (k n) -> p k n", k=4) for m in range(4)]
        WTL = [halves(f"wtl{m}", 2048 * m, 2048)[:, :].rearrange("p (k n) -> p k n", k=4) for m in range(4)]
        XTH = [halves(f"xth{i}", xt_at + 512 * i, 512)[:, :].rearrange("p (k t) -> p k t", k=4) for i in range(2)]
        XTL = [halves(f"xtl{i}", xt_at + 1024 + 512 * i, 512)[:, :].rearrange("p (k t) -> p k t", k=4)
               for i in range(2)]
        QBH, QBL = (halves(f"qb{i}", at, 2048)[:, :].rearrange("p (g r t) -> p g r t", g=4, r=4)
                    for i, at in enumerate((qb_at, qbl_at)))
        KTH, KTL = (halves(f"kt{i}", b_at + 512 * i, 512)[:, :] for i in range(2))
        ATH, ATL = (halves(f"at{i}", ath_at + 512 * i, 512)[:, :] for i in range(2))
        Ks = [halves(f"keys{i}", k_at + 512 * i, 512, F)[:, :] for i in range(2)]
        KH, KL = (halves(f"kh{i}", kh_at + 512 * i, 512)[:, :] for i in range(2))
        UPTO, AFTER = (halves(f"tri{i}", tri_at + 128 * i, 128)[:, :] for i in range(2))

        f = Area(xn3_at)
        HG = [f.take(512) for _ in range(2)]
        HT = [f.take(512) for _ in range(2)]
        PT = [f.take(512) for _ in range(2)]
        WLS = [halves(f"wls{i}", f.at + 512 * i, 512)[:, :] for i in range(2)]
        wst = Area(qb_at)
        WST = [wst.take(2048).rearrange("p (k n) -> p k n", k=4) for _ in range(2)]
        GW = WST[0][0:32, 0, :]
        fx = Area(wth_at)
        FX = [fx.take(512) for _ in range(20)]
        XT4 = [big[:, obd_at + 2048 * i:obd_at + 2048 * i + 2048].rearrange("p (k t) -> p k t", k=4) for i in range(2)]
        fx = Area(qb_at)
        FX += [fx.take(512) for _ in range(8)]
        NF0 = len(FX)
        for at in (3 * 4096, 0):
            fx = Area(at)
            FX += [fx.take(512) for _ in range(8)]
        NF = len(FX)
        XLA = [t[:, at:at + 2048].rearrange("p (t d) -> p t d", t=4)
               for t, at in [(big, wth_at + 2048 * i) for i in range(4)] + [(big2, 2048 * i) for i in range(3)]
               + [(big2, qb_at - CUT), (big2, qb_at + 2048 - CUT)]]
        NX4 = len(XLA)
        TILES = [[XLA[n // 4][:, n % 4, :] for n in range(4 * NX4)], XN3]

        ST6 = [SM[:, 8 * i:8 * i + 6] for i in range(4)]
        MV = [SM[:, 32 + 4 * i:34 + 4 * i] for i in range(4)]
        VE = [SM[:, 48 + i:49 + i] for i in range(4)]
        RS = [SM[:, 52 + i:53 + i] for i in range(4)]
        NHALF = SM[:, 56:57]
        GB = SM[:, 57:58]
        T8 = SM[:, 64:72]
        NMX = SM[:, 72:73]
        SUM = SM[:, 73:74]
        RSUM = SM[:, 74:75]
        DEN = SM[:, 80:96]
        RDEN = SM[:, 96:112]
        MVG = [SM[:, 112 + 8 * i:120 + 8 * i].rearrange("p (t m) -> p t m", m=2) for i in range(2)]
        VEG, RSG, NMG = ([SM[:, at + 4 * i:at + 4 + 4 * i] for i in range(2)] for at in (128, 136, 144))

        pe, dve, act, pool = (Queue(sem(n)) for n in ("s_pe", "s_dve", "s_act", "s_pool"))
        sp = Queue(sem("s_sp"))

        def counter(name):
            return [sem(name), 0]

        c_ring = [counter(f"c_ring{i}") for i in range(8)]
        c_x = [counter(f"c_x{i}") for i in range(9)]
        c_x2 = [counter(f"c_x2{i}") for i in range(2)]
        c_fl = [counter(f"c_fl{i}") for i in range(NF)]
        c_fs = [counter(f"c_fs{i}") for i in range(NF)]
        c_wst = [counter(f"c_wst{i}") for i in range(2)]
        c_b1, c_b2, c_bias, c_gb, c_gw = (counter(n) for n in ("c_b1", "c_b2", "c_bias", "c_gb", "c_gw"))

        free = [None] * 8

        def mm(o, l, r, start, stop):
            return lambda e: nc.tensor.matmul(o, l, r, start=start, stop=stop, skip_group_check=True)

        def tr(o, i, n=128):
            return lambda e: nc.tensor.transpose(o, i, IDN[0:n, 0:n])

        def copy_act(o, i):
            return lambda e: nc.scalar.copy(o, i)

        def tt(o, p, q, op):
            return lambda e: nc.vector.tensor_tensor(o, p, q, op)

        def const(o, v):
            return pool(lambda e: nc.gpsimd.memset(o, v), (pool.sem, pool.count))

        const(IDN, 0.0)
        const(TRI, 1.0)
        const(MBD, 0.0)
        const(SEL, 0.0)
        const(NHALF, -0.5)
        const(MG[:, :, 256:280], 0.0)

        def select(t, pattern, cm, base, op, fill):
            return pool(lambda e: nc.gpsimd.affine_select(out=t, in_=t, compare_op=op, fill=fill, base=base,
                                                          pattern=pattern, channel_multiplier=cm),
                        (pool.sem, pool.count))

        t_idn = select(IDN, [[-1, 128]], 1, 0, ALU.not_equal, 1.0)
        select(TRI, [[1, 128]], -1, 0, ALU.is_ge, 0.0)
        for r in range(4):
            t_cst = pool(lambda e, r=r: nc.gpsimd.memset(MBD[32 * r:32 * r + 32, 32 * r:32 * r + 32], 1.0),
                         (pool.sem, pool.count))
        for j in range(4):
            t_cst = select(SEL[:, 0:287], [[-1, 287]], 32, 31 - 1024 * j, ALU.not_equal, 1.0)

        t_tri = act(copy_act(UPTO, TRI), t_cst)
        t_tri = act(lambda e: nc.scalar.activation(AFTER, TRI, ACT.Identity, scale=-1.0, bias=1.0), t_cst)

        ring_tok, ring_free = {}, [None] * 8

        def slot_of(g):
            if g < 4 * E:
                return g if g < 7 else (g + 1) % 4
            return {4 * E: 0, 4 * E + 1: 7}.get(g, (g - 1) % 4)

        def after_chunk(g):
            if g < 4 * E:
                nxt = g + 7 if g < 4 else None if g < 7 else g + 4
            else:
                nxt = g + 5 if g == 4 * E else None if g == 4 * E + 1 else g + 4
            return nxt if nxt is not None and (nxt < 4 * E) == (g < 4 * E) and nxt < 8 * E else None

        def load_chunk(g, *waits):
            e, part = (g // 4) % E, g % 4
            slot = slot_of(g)
            if part < 2:
                src = w1[e, 0:512, :].rearrange("(p k) n -> p k n", k=4)[:, 2 * part:2 * part + 2, :]
                dst = ring[slot].rearrange("p (k n) -> p k n", k=2)
            else:
                src = w2[e, 0:2048, :].rearrange("(j c i) n -> c j (i n)", j=4, i=4)[:, 2 * part - 4:2 * part - 2, :]
                dst = ring[slot].rearrange("p (j n) -> p j n", j=2)
            ring_tok[g] = sp.dma(c_ring[slot], dst, src, ring_free[slot], *waits)

        ln_n, mv_free = [0], [None] * 4

        def stats(src, src_tok):
            i = ln_n[0] % 4
            ln_n[0] += 1
            t = dve(lambda e: nc.vector.bn_stats(ST6[i], src), src_tok)
            t = dve(lambda e: nc.vector.bn_aggr(MV[i], ST6[i]), t, mv_free[i])
            t = dve(lambda e: nc.vector.tensor_scalar(VE[i], MV[i][:, 1:2], EPS, None, ALU.add), t)
            return i, pool(lambda e: nc.gpsimd.tensor_tensor(RS[i], VE[i], NHALF, ALU.pow), t)

        def apply(stat, src, dst, *waits):
            i, t = stat
            mv_free[i] = dve(lambda e: nc.vector.tensor_scalar(dst, src, MV[i][:, 0:1], RS[i], ALU.subtract, ALU.mult),
                           t, *waits)
            return mv_free[i]

        order = list(range(8))

        def bank(among=range(8)):
            k = next(k for k in order if k in among)
            order.remove(k)
            order.append(k)
            return k

        ANY, NOT_S = (0, 1, 4, 5, 6, 7), (0, 1)
        banks, tbanks = [range(8)], [range(8)]

        xt3_free = [None, None]
        logit_tok = {}
        mt_free = [None]
        l_free = [None] * 4
        xt3_tok = {}

        def gate_transpose(n, src, tok):
            k = bank(tbanks[0])
            for j in range(4):
                t = pe(tr(ps[:, k, 128 * j:128 * j + 128], src[:, 128 * j:128 * j + 128]),
                       tok, free[k], t_idn, inc=j == 3)
            i = n % 2
            free[k] = xt3_tok[n] = act(copy_act(XT3[i], ps[:, k, :].rearrange("p (k t) -> p k t", k=4)),
                                       t, xt3_free[i])

        def gate_logits(n):
            b, c, i = n // 8, n % 8, n % 2
            q = 32 * (b % 4)
            k = bank(banks[0])
            for j in range(4):
                t = pe(mm(ps[q:q + 32, k, 0:128], GT[:, j, :], XT3[i][:, j, :], j == 0, j == 3),
                       xt3_tok[n], free[k], t_gt, inc=j == 3)
            xt3_free[i] = t
            free[k] = logit_tok[n] = act(
                lambda e: nc.scalar.activation(L[q:q + 32, 128 * c:128 * c + 128], ps[q:q + 32, k, 0:128],
                                               ACT.Identity, bias=GB[q:q + 32, :]), t, t_gb, l_free[b % 4])

        def gate_max(b):
            R_ = slice(32 * (b % 4), 32 * (b % 4) + 32)
            return dve(lambda e: nc.vector.max(T8[R_, :], L[R_, :]), logit_tok[8 * b + 7])

        def gate_replace(b, m, tok):
            R_ = slice(32 * (b % 4), 32 * (b % 4) + 32)
            W = M[m][R_, b // 4, :]
            t2 = dve(lambda e: nc.vector.match_replace(W, T8[R_, :], L[R_, :], LOWEST), tok)
            t = dve(lambda e: nc.vector.tensor_scalar(NMX[R_, :], T8[R_, 0:1], -1.0, None, ALU.mult), tok)
            return t, t2

        def gate_exp(b, m, toks):
            R_ = slice(32 * (b % 4), 32 * (b % 4) + 32)
            W = M[m][R_, b // 4, :]
            t2 = dve(tt(W, L[R_, :], W, ALU.not_equal), toks[1])
            return act(lambda e: nc.scalar.activation(L[R_, :], L[R_, :], ACT.Exp, bias=NMX[R_, :],
                                                      accum_out=SUM[R_, :]), toks[0], t2), t2

        def topk(b, m):
            return gate_exp(b, m, gate_replace(b, m, gate_max(b)))

        def weights(b, m, toks):
            q = 32 * (b % 4)
            R_ = slice(q, q + 32)
            W = M[m][R_, b // 4, :]
            t = dve(lambda e: nc.vector.reciprocal(RSUM[R_, :], SUM[R_, :]), toks[0])
            l_free[b % 4] = t = dve(lambda e: nc.vector.scalar_tensor_tensor(
                out=W, in0=L[R_, :], scalar=RSUM[R_, :], in1=W, op0=ALU.mult, op1=ALU.mult), t, toks[1])
            return t

        def merge_transpose(b, m, tok):
            q = 32 * (b % 4)
            k = bank(banks[0])
            for c in range(8):
                t = pe(lambda e, c=c: nc.tensor.transpose(ps[:, k, 32 * c:32 * c + 32],
                                                          M[m][q:q + 32, b // 4, 128 * c:128 * c + 128],
                                                          IDN[q:q + 32, q:q + 32]), tok, free[k], inc=c == 7)
            free[k] = t = act(copy_act(MT, ps[:, k, 0:256].rearrange("p (c e) -> p c e", c=8)), t, mt_free[0])
            return t

        def merge_tokens(b, m, tok, xn_tok):
            k = bank(banks[0])
            for h in range(2):
                for c in range(4):
                    t = pe(mm(ps[32 * c:32 * c + 32, k, :], MT[:, 4 * h + c, :], TILES[m][(8 * b + 4 * h + c) % len(TILES[m])],
                              h == 0, h == 1), tok, xn_tok, free[k], inc=h == 1 and c == 3)
            mt_free[0] = merged[b + 8 * m] = t
            free[k] = t = act(copy_act(PR3, ps[:, k, :]), t, pr3_free[0])
            return t

        def merge_end(b, tok):
            k = bank(banks[0])
            for j in range(4):
                t = pe(tr(ps[:, k, 128 * j:128 * j + 128], PR3.rearrange("p (c k) -> p k c", k=4)[:, j, :]),
                       tok, free[k], inc=j == 3)
            pr3_free[0] = t
            free[k] = mg_tok[b] = dve(lambda e: nc.vector.tensor_reduce(
                MG[:, :, 0:256].rearrange("p k (e b) -> p k e b", b=8)[:, :, :, b],
                ps[:, k, :].rearrange("p (k q e) -> p k e q", k=4, q=4), AX.X, ALU.add), t, mg_free[0])

        pend = {}

        merged = {}
        pr3_free = [None]
        mg_tok, mg_free = {}, [None]

        t_gw = sp.dma(c_gw, GW, gate_w)
        for r in range(4):
            t_gb = sp.dma(c_gb, GB[32 * r:32 * r + 32, :], gate_b.rearrange("(e a) -> e a", a=1))
        xl_tok, xl_free = {}, [None] * 4

        def load_x(g, *waits):
            xl_tok[g] = sp.dma(c_x[g % NX4], XLA[g % NX4], xs[4 * g:4 * g + 4].rearrange("t p d -> p t d"), *waits)

        for g in range(7):
            load_x(g)
        k = bank()
        for j in range(4):
            t = pe(lambda e, j=j, k=k: nc.tensor.transpose(ps[:, k, 32 * j:32 * j + 32], GW[:, 128 * j:128 * j + 128],
                                                      IDN[0:32, 0:32]), t_gw, t_idn, inc=j == 3)
        free[k] = t_gt = act(copy_act(GT, ps[:, k, 0:128].rearrange("p (k e) -> p k e", k=4)), t)

        for g in range(7, NX4):
            load_x(g, t_gt)

        xn_tok, stat = {}, {}
        NG = NT // 4
        rs_tok, nm_tok, norm_tok, xt4_tok, xt4_free = {}, {}, {}, {}, [None] * 2
        def stats4(g):
            i = g % 2
            ts = []
            for j in range(4):
                ts.append(dve(lambda e, j=j: nc.vector.bn_stats(ST6[j], XLA[g % NX4][:, j, :]), xl_tok[g]))
            for j in range(4):
                t = dve(lambda e, j=j: nc.vector.bn_aggr(MVG[i][:, j, :], ST6[j]), ts[j])
            t = dve(lambda e: nc.vector.tensor_scalar(VEG[i], MVG[i][:, :, 1], EPS, None, ALU.add), t)
            rs_tok[g] = pool(lambda e: nc.gpsimd.tensor_tensor(RSG[i], VEG[i], NHALF.broadcast_to([128, 4]), ALU.pow),
                             t, nm_tok.get(g - 2), norm_tok.get(g - 2))

        def norm_mean(g):
            i = g % 2
            nm_tok[g] = dve(lambda e: nc.vector.scalar_tensor_tensor(
                out=NMG[i], in0=MVG[i][:, :, 0], scalar=-1.0, in1=RSG[i], op0=ALU.mult, op1=ALU.mult), rs_tok[g],
                norm_tok.get(g - 2))

        def norm(g, j):
            i = g % 2
            norm_tok[g] = xn_tok[4 * g + j] = act(lambda e: nc.scalar.activation(
                XLA[g % NX4][:, j, :], XLA[g % NX4][:, j, :], ACT.Identity, bias=NMG[i][:, j:j + 1],
                scale=RSG[i][:, j:j + 1]), nm_tok[g])

        def transposed(g, j):
            i, n = g % 2, 4 * g + j
            k = bank()
            for m in range(4):
                t = pe(tr(ps[:, k, 128 * m:128 * m + 128], XLA[g % NX4][:, j, 128 * m:128 * m + 128]),
                       xn_tok[n], free[k], t_idn, inc=m == 3)
            dst = XT4[i][:, :, 128 * j:128 * j + 128]
            src = ps[:, k, :].rearrange("p (k t) -> p k t", k=4)
            if j == 3 or (j == 1 and g % 2 == 0):
                free[k] = xt4_tok[n] = dve(lambda e: nc.vector.tensor_copy(dst, src), t, xt4_free[i])
            else:
                free[k] = xt4_tok[n] = act(copy_act(dst, src), t, xt4_free[i])

        def logits4(g):
            b, i = g // 2, g % 2
            q = 32 * (b % 4)
            k = bank()
            for j in range(4):
                t = pe(mm(ps[q:q + 32, k, :], GT[:, j, :], XT4[i][:, j, :], j == 0, j == 3),
                       xt4_tok[4 * g + 2], xt4_tok[4 * g + 3], free[k], t_gt, inc=j == 3)
            xt4_free[i] = t
            free[k] = logit_tok[4 * g + 3] = act(
                lambda e: nc.scalar.activation(L[q:q + 32, 512 * i:512 * i + 512], ps[q:q + 32, k, :],
                                               ACT.Identity, bias=GB[q:q + 32, :]), t, t_gb, l_free[b % 4])

        def batch(g, after):
            b = (g - after) // 2
            return [b] if (g - after) % 2 == 0 and 0 <= b < B else []

        for g in range(-2, NG + 5):
            if 0 <= g + 1 < NG:
                norm_mean(g + 1)
            if g + 2 < NG:
                stats4(g + 2)
            for b in batch(g, 4):
                pend[b] = weights(b, 0, pend[b])
            for b in batch(g, 6):
                merge_end(b, pend[b])
            for j in range(4):
                if 0 <= g < NG:
                    transposed(g, j)
                if 0 <= g + 1 < NG:
                    norm(g + 1, j)
            if 0 <= g - 1 < NG:
                logits4(g - 1)
            for b in batch(g, 4):
                pend[b] = merge_transpose(b, 0, pend[b])
            for b in batch(g, 5):
                pend[b] = merge_tokens(b, 0, pend[b], xn_tok[8 * b + 7])
                for n in (2 * b + NX4, 2 * b + 1 + NX4):
                    if n < NG:
                        load_x(n, merged[b])
            for b in batch(g, 3):
                pend[b] = topk(b, 0)
            if g in (7, 9, 11, 13):
                load_chunk((g - 7) // 2)
            elif g == 14:
                load_chunk(4)
            elif g in (15, 17):
                b = (g - 5) // 2
                load_chunk(b, merged[b])
        obd0_tok = [None]
        obd0_tok[0] = pool(lambda e: nc.gpsimd.memset(big[:, obd_at:obd_at + 4096], 0.0), xt4_free[0], xt4_free[1])

        def experts(first, extra):
            hb, tb, pb = {}, {}, {}
            h_tok, hg_tok, ht_tok, pt_tok, hgf, htf, ptf = {}, {}, {}, {}, [None] * 2, [None] * 2, [None] * 2
            o_last = None
            for e in range(E + 1):
                if e < E:
                    g = first + 4 * e
                    i = e % 2
                    k = i
                    for j in range(4):
                        r = 32 * j + e
                        pe(mm(ps[32 * j:32 * j + 32, k, :], IDN[:, r:r + 1].broadcast_to([128, 32]), B1,
                              True, False), free[k], t_b1, mg_tok[7], inc=False)
                    for kt in range(4):
                        v = ring[slot_of(g + kt // 2)].rearrange("p (k n) -> p k n", k=2)
                        for j in range(4):
                            t = pe(mm(ps[32 * j:32 * j + 32, k, :], MG[:, kt, 8 * e:8 * e + 32],
                                      v[:, kt % 2, 512 * j:512 * j + 512], False, kt == 3),
                                   ring_tok[g + kt // 2], inc=kt % 2 == 1 and j == 3)
                        if kt % 2 == 1:
                            ring_free[slot_of(g + kt // 2)] = t
                            nxt_chunk = after_chunk(g + kt // 2)
                            if nxt_chunk is not None:
                                load_chunk(nxt_chunk)
                    mg_free[0] = t
                    free[k] = t = act(lambda q, i=i, k=k: nc.scalar.activation(HG[i], ps[:, k, :], ACT.Gelu),
                                      t, hgf[i])
                    hg_tok[e] = t
                if e >= 1:
                    p = e - 1
                    i = p % 2
                    for half in range(2):
                        off = 128 * half + 31 - p
                        t = pe(mm(ps[:, 6 + half, :], SEL[:, off:off + 128], PT[i], p == 0, p == E - 1),
                               pt_tok[p], free[6 + half], t_cst)
                    ptf[i] = o_last = t
                if e < E:
                    i = e % 2
                    k = 2 + i
                    for q in range(4):
                        t = pe(tr(ps[:, k, 128 * q:128 * q + 128],
                                  HG[i].rearrange("p (c t) -> p t c", t=4)[:, q, :]),
                               hg_tok[e], free[k], inc=q == 3)
                    hgf[i] = t
                    free[k] = t = dve(lambda q, i=i, k=k: nc.vector.tensor_copy(HT[i], ps[:, k, :]), t, htf[i])
                    k = 4 + i
                    for j in range(4):
                        v = ring[slot_of(g + 2 + j // 2)].rearrange("p (j i n) -> p j i n", j=2, i=4)
                        for q in range(4):
                            t2 = pe(mm(ps[32 * q:32 * q + 32, k, :], HT[i][:, 128 * q + 32 * j:128 * q + 32 * j + 32],
                                       v[:, j % 2, q, :], j == 0, j == 3),
                                    t, free[k], ring_tok[g + 2 + j // 2], inc=j % 2 == 1 and q == 3)
                        if j % 2 == 1:
                            ring_free[slot_of(g + 2 + j // 2)] = t2
                            nxt_chunk = after_chunk(g + 2 + j // 2)
                            if nxt_chunk is not None:
                                load_chunk(nxt_chunk)
                    htf[i] = t2
                    free[k] = pt_tok[e] = act(copy_act(PT[i], ps[:, k, :]), t2, ptf[i])
                    extra(e)
            toks = []
            for b in range(B):
                q = 32 * (b % 4)
                R = slice(q, q + 32)
                toks.append(dve(tt(OBD[R, b, :], ps[R, 6 + b // 4, :], B2[R, :], ALU.add), o_last, t_b2, obd0_tok[0],
                                obd_free[0]))
            free[6] = free[7] = toks[-1]
            return toks

        obd_free = [None]

        def load_biases(*waits):
            for j in range(4):
                t = sp.dma(c_b1, B1[32 * j:32 * j + 32, :], w1[:, 512, 512 * j:512 * j + 512], *waits)
                t2 = sp.dma(c_b2, B2[32 * j:32 * j + 32, :], w2[:, 2048, :], *waits)
            return t, t2

        t_b1, t_b2 = load_biases()
        for t_, s_ in ((BQ, bq), (BK, bk), (BV, bv), (BO, bo)):
            t_bias = sp.dma(c_bias, t_, s_.partition_broadcast(128))

        wl_tok, wls_free = [None], [None] * 2
        c_wls = [counter(f"c_wls{i}") for i in range(2)]
        c_wl = counter("c_wl")
        wst_free = [t_gt, None]
        wst_tok = {}

        def prepare(e):
            if e % 6 == 0 and e < 24:
                m = e // 6
                wst_tok[m] = act.dma(c_wst[m % 2], WST[m % 2],
                                     (Wq, Wk, Wv, Wo)[m].rearrange("(o p) i -> p o i", p=128), wst_free[m % 2])
            m, kt = e // 6, e % 6 - 1
            if 0 <= kt < 4 and m < 4:
                k = 2 + (e + 1) % 2
                for o in range(4):
                    t = pe(tr(ps[:, k, 128 * o:128 * o + 128], WST[m % 2][:, o, 128 * kt:128 * kt + 128]),
                           wst_tok[m], free[k], inc=o == 3)
                wst_free[m % 2] = t
                t = act(copy_act(WTH[m][:, kt, :], ps[:, k, :]), t, ring_free[5], ring_free[6])
                i = (4 * m + kt) % 2
                free[k] = t = dve(tt(WLS[i], ps[:, k, :], WTH[m][:, kt, :].bitcast(F), ALU.subtract), t, wls_free[i])
                wl_tok[0] = wls_free[i] = act.dma(c_wls[i], wl[m, kt], WLS[i].bitcast(F), t)

        o_tok = experts(0, prepare)
        for m in range(4):
            t_w = sp.dma(c_wl, WTL[m].bitcast(F), wl[m].rearrange("k p n -> p k n"),
                         wls_free[0], wls_free[1], ring_free[0], ring_free[1])

        fl_tok, fs_tok = {}, {}

        def load_f(n, *waits, on=sp):
            fl_tok[n] = on.dma(c_fl[n % NF], FX[n % NF], x2s[n], fs_tok.get(n - NF), x2_tok[n], *waits)

        x1_tok, x1b_tok, x2_tok, xnt_tok, xt_tok = {}, {}, {}, {}, {}
        q_tok, k_tok, v_tok = {}, {}, {}
        x1_free, x2_free, xnf, xtf = [None] * 4, [None] * 2, [None], [None] * 2
        kf, vf = [[], []], [[], []]
        once = {n_: None for n_ in ("KT", "QT", "QB", "AT", "KV", "TMP", "KH", "ST")}
        kv_tok = pr_tok = None
        pool(lambda e: nc.gpsimd.memset(QBL.bitcast(F), 0.0), ring_free[4])
        z_qb = pool(lambda e: nc.gpsimd.memset(QBH.bitcast(F), 0.0), wst_free[0], wst_free[1])

        def residual(n):
            b, c = n // 8, n % 8
            k = bank(ANY)
            t = pe(mm(ps[:, k, :], M[0][:, b // 4, 128 * c:128 * c + 128], OBD[:, b, :], True, True),
                   free[k], o_tok[b], o_tok[7])
            obd_free[0] = t
            i = n % 4
            free[k] = x1_tok[n] = dve(
                lambda e: nc.vector.scalar_tensor_tensor(out=X1[i], in0=ps[:, k, :], scalar=0.5, in1=X1[i],
                                                         op0=ALU.mult, op1=ALU.add), t, xl_tok[NT + n])
            stat[n] = stats(X1[i], x1_tok[n])

        def x_apply(n):
            i = n % 4
            xnt_tok[n] = apply(stat[n], X1[i], XN, xnf[0])
            x1b_tok[n] = pool(lambda e: nc.gpsimd.tensor_tensor(X1[i], X1[i], BO, ALU.add), xnt_tok[n], t_bias)

        def load_x1(n):
            i = n % 4
            xl_tok[NT + n] = sp.dma(c_x[i], X1[i], xs[n], x1_free[i], ring_free[2], ring_free[3])

        def x_transpose(n):
            k, i = bank(NOT_S), n % 2
            for j in range(4):
                t = pe(tr(ps[:, k, 128 * j:128 * j + 128], XN[:, 128 * j:128 * j + 128]),
                       xnt_tok[n], free[k], inc=j == 3)
            xnf[0] = t
            v = ps[:, k, :].rearrange("p (k t) -> p k t", k=4)
            t = act(copy_act(XTH[i], v), t, xtf[i])
            free[k] = xt_tok[n] = dve(tt(XTL[i], v, XTH[i].bitcast(F), ALU.subtract), t)

        def project(n, w, dst, bias, exp, waits):
            k, i = bank(NOT_S if w == 2 else ANY), n % 2
            for j in range(4):
                pe(mm(ps[:, k, :], XTH[i][:, j, :], WTH[w][:, j, :], j == 0, False), xt_tok[n], free[k], t_w, inc=False)
                pe(mm(ps[:, k, :], XTH[i][:, j, :], WTL[w][:, j, :], False, False), inc=False)
                t = pe(mm(ps[:, k, :], XTL[i][:, j, :], WTH[w][:, j, :], False, j == 3), inc=j == 3)
            if w == 2:
                xtf[i] = t
            free[k] = t = dve(tt(dst, ps[:, k, :], bias, ALU.add), t, t_bias, *waits)
            if exp:
                t = act(lambda e: nc.scalar.activation(dst, dst, ACT.Exp), t)
            return t

        def h4(t):
            return t.rearrange("p (g n) -> p g n", g=4)

        for n in range(4):
            load_x1(n)
        banks[0], tbanks[0] = ANY, NOT_S
        for n in range(-3, NT + 6):
            live = 0 <= n < NT
            nxt = 0 <= n + 1 < NT
            if live:
                b, c, i = n // 8, n % 8, n % 2
                if c < 7:
                    pe(mm(ps[:, 2, :], AFTER, KH, False, False), pr_tok, inc=False)
                    once["KH"] = pe(mm(ps[:, 2, :], AFTER, KL, False, False))
            if 0 <= n + 2 < NT:
                residual(n + 2)
            if 4 <= n + 3 < NT:
                load_x1(n + 3)
            if live:
                k = bank((4, 5, 6, 7))
                for g in range(4):
                    t = pe(tr(ps[:, k, 128 * g:128 * g + 128], Ks[i][:, 128 * g:128 * g + 128]), free[k], k_tok[n],
                           inc=g == 3)
                t = act(copy_act(KTH, ps[:, k, :]), t, once["KT"])
                free[k] = kt_tok = dve(tt(KTL, ps[:, k, :], KTH.bitcast(F), ALU.subtract), t, once["KT"])
                k = bank((4, 5, 6, 7))
                for g in range(4):
                    t = pe(tr(ps[:, k, 128 * g:128 * g + 128], Qs[i][:, 128 * g:128 * g + 128]), free[k], qh_tok,
                           inc=g == 3)
                qt_tok = act(copy_act(QT, ps[:, k, :]), t, once["QT"])
                tqs = []
                for r in range(4):
                    R_ = slice(32 * r, 32 * r + 32)
                    v = ps[R_, k, :].rearrange("p (g t) -> p g t", g=4)
                    tq = act(copy_act(QBH[R_, :, r, :], v), t, once["QB"], z_qb)
                    tqs.append((tt(QBL[R_, :, r, :], v, QBH[R_, :, r, :].bitcast(F), ALU.subtract), tq, once["QB"]))
                dve(*tqs[0])
                dve(*tqs[1])
                qt_bank = k
            if nxt:
                q_tok[n + 1] = project(n + 1, 0, Qs[(n + 1) % 2], BQ, True, [])
            if 0 <= n + 2 < NT:
                x_apply(n + 2)
            if live:
                dve(*tqs[2])
                free[qt_bank] = tql = dve(*tqs[3])
            if nxt:
                j = (n + 1) % 2
                k_tok[n + 1] = project(n + 1, 1, Ks[j], BK, True, kf[j])
                t = act(copy_act(KH, Ks[j]), k_tok[n + 1], once["KH"])
                kh_tok = pool(lambda e, j=j: nc.gpsimd.tensor_tensor(KL, Ks[j], KH.bitcast(F), ALU.subtract),
                              t, once["KH"])
                kf[j] = [kh_tok]
            if n >= 1 and n - 1 < NT:
                xn_tok[n - 1] = apply(x2_stat, X2, XN3[(n - 1) % NX], merged.get(8 + (n - 1 - NX) // 8 if n > NX else None))
                x2_free[1] = xn_tok[n - 1]
            if 0 <= n + 2 < NT:
                x_transpose(n + 2)
            if live:
                s_tok = []
                for g in range(4):
                    pe(mm(ps[:, 4 + g, :], h4(KTH)[:, g, :], QBH[:, g, :, :], True, False),
                       free[4 + g], kt_tok, tq, inc=False)
                    pe(mm(ps[:, 4 + g, :], h4(KTH)[:, g, :], QBL[:, g, :, :], False, False), tql, inc=False)
                    s_tok.append(pe(mm(ps[:, 4 + g, :], h4(KTL)[:, g, :], QBH[:, g, :, :], False, True)))
                once["KT"] = once["QB"] = s_tok[3]
                for g in range(4):
                    free[4 + g] = st_tok = dve(tt(h4(ST[:, g, :]), h4(ps[:, 4 + g, :]),
                                                  TRI.unsqueeze(1).broadcast_to([128, 4, 128]), ALU.mult),
                                               s_tok[g], once["ST"])
            if 1 <= n <= NT:
                gate_transpose(n - 1, XN3[(n - 1) % NX], xn_tok[n - 1])
            if nxt:
                v_tok[n + 1] = project(n + 1, 2, Vs[(n + 1) % 2], BV, False, vf[(n + 1) % 2])
            gb, done = divmod(n - 9, 8)
            if n < 9:
                done = None
            if done == 0:
                pend[gb] = gate_max(gb)
            elif done == 1:
                pend[gb] = gate_replace(gb, 1, pend[gb])
            elif done == 2:
                pend[gb] = gate_exp(gb, 1, pend[gb])
            elif done == 3:
                pend[gb] = weights(gb, 1, pend[gb])
            if live:
                for g in range(4):
                    if c:
                        ti = pe(mm(ps[:, 3, 128 * g:128 * g + 128], h4(KV)[:, g, :], h4(QT)[:, g, :], True, False),
                                free[3], kv_tok, qt_tok, inc=g == 3)
                    for r in range(4):
                        o = ps[32 * r:32 * r + 32, 3, 128 * g:128 * g + 128]
                        t = pe(mm(o, Vs[i][:, 128 * g + 32 * r:128 * g + 32 * r + 32],
                                  ST[:, g, 128 * r:128 * r + 128], c == 0, True), free[3], st_tok, v_tok[n],
                               inc=g == 3 and r == 3)
                once["ST"] = once["QT"] = t
                if c:
                    once["KV"] = ti
                t = act(copy_act(ATH, ps[:, 3, :]), t, once["AT"])
                free[3] = at_tok = dve(tt(ATL, ps[:, 3, :], ATH.bitcast(F), ALU.subtract), t)
            if nxt:
                j, first = (n + 1) % 2, (n + 1) % 8 == 0
                pe(mm(ps[:, 2, :], UPTO, KH, first, False), kh_tok, t_tri, pr_tok, inc=False)
                once["KH"] = t = pe(mm(ps[:, 2, :], UPTO, KL, False, False))
                pr_tok = t = dve(tt(PR, ps[:, 2, :], Qs[j], ALU.mult), t, q_tok[n + 1], once["TMP"])
                t = dve(lambda e: nc.vector.tensor_reduce(DEN, PR.rearrange("p (h d) -> p h d", h=16),
                                                          AX.X, ALU.add), t)
                t = dve(lambda e: nc.vector.reciprocal(RDEN, DEN), t)
                qh_tok = dve(tt(Qs[j].rearrange("p (h d) -> p h d", h=16), Qs[j].rearrange("p (h d) -> p h d", h=16),
                                RDEN.unsqueeze(2).broadcast_to([128, 16, 32]), ALU.mult), t)
            if live and c < 7:
                k = bank(ANY)
                for g in range(4):
                    t = pe(mm(ps[:, k, 128 * g:128 * g + 128], Ks[i][:, 128 * g:128 * g + 128],
                              Vs[i][:, 128 * g:128 * g + 128], True, True), free[k], inc=g == 3)
                dst = KV if c == 0 else TMP
                free[k] = kv_tok = dve(tt(h4(dst), h4(ps[:, k, :]), MBD.unsqueeze(1).broadcast_to([128, 4, 128]),
                                          ALU.mult), t, once["KV"], once["TMP"])
                if c:
                    kv_tok = once["TMP"] = pool(lambda e: nc.gpsimd.tensor_tensor(KV, KV, TMP, ALU.add), kv_tok)
            if live:
                t = (pe.sem, pe.count)
                kf[i] = kf[i] + [t]
                vf[i] = [t]
            if done == 3:
                pend[gb] = merge_transpose(gb, 1, pend[gb])
            if live:
                k = bank(ANY)
                for g in range(4):
                    pe(mm(ps[:, k, :], h4(ATH)[:, g, :], WTH[3][:, g, :], g == 0, False), free[k], at_tok, inc=False)
                    pe(mm(ps[:, k, :], h4(ATH)[:, g, :], WTL[3][:, g, :], False, False), inc=False)
                    t = pe(mm(ps[:, k, :], h4(ATL)[:, g, :], WTH[3][:, g, :], False, g == 3), inc=g == 3)
                once["AT"] = t
                j = n % 4
                free[k] = x1_free[j] = t = dve(tt(X2, ps[:, k, :], X1[j], ALU.add), t, x1b_tok[n], x2_free[0], x2_free[1])
                x2_free[0] = x2_tok[n] = sp.dma(c_x2[i], x2s[n], X2, t)
                x2_stat = stats(X2, t)
            if 1 <= n <= NT:
                gate_logits(n - 1)
            if done == 3:
                pend[gb] = merge_tokens(gb, 1, pend[gb], xn_tok[8 * gb + 7])
            elif done == 4:
                merge_end(gb, pend[gb])
            if n == NT - 2:
                load_chunk(128, (pe.sem, pe.count))
                load_chunk(129, (pe.sem, pe.count))
                for m in range(16, 20):
                    load_f(m, (pe.sem, pe.count))
            if n == NT - 1:
                att = [(pe.sem, pe.count), (dve.sem, dve.count), (pool.sem, pool.count), (act.sem, act.count)]
                load_chunk(130, *att)
                t_b1, t_b2 = load_biases(*att)
                for m in range(10):
                    load_f(m, *att)
            if n == NT:
                for g in range(131, 133):
                    load_chunk(g, x2_free[0], xn_tok[NT - 1])
                for m in (*range(10, 16), *range(20, NF0)):
                    load_f(m, *att)

        def clear(e):
            if e == 0:
                obd0_tok[0] = pool(
                    lambda q: nc.gpsimd.memset(big[:, obd_at:obd_at + 4096], 0.0), ring_free[7])

        o_tok = experts(128, clear)
        for n in range(NF0, NF):
            load_f(n, ring_free[slot_of(252)], ring_free[slot_of(253)])
        for n in range(NT):
            b, c, i = n // 8, n % 8, n % NF
            k = n % 6
            t = pe(mm(ps[:, k, :], M[1][:, b // 4, 128 * c:128 * c + 128], OBD[:, b, :], True, True),
                   free[k], o_tok[b], o_tok[7])
            free[k] = t = dve(lambda e, i=i, k=k: nc.vector.scalar_tensor_tensor(
                out=FX[i], in0=ps[:, k, :], scalar=0.5, in1=FX[i], op0=ALU.mult, op1=ALU.add), t, fl_tok[n])
            fs_tok[n] = sp.dma(c_fs[i], outs[n], FX[i], t)
            if n >= 4 and n - 4 + NF < NT:
                load_f(n - 4 + NF, on=act)
        sp.wait(*[fs_tok[n] for n in range(NT - NF, NT)])

        block = ctx.enter_context(nc.Block())

        @block.sync
        def _(eng):
            sp.issue(eng)

        @block.gpsimd
        def _(eng):
            pool.issue(eng)

        @block.scalar
        def _(eng):
            act.issue(eng)

        @block.vector
        def _(eng):
            dve.issue(eng)

        @block.tensor
        def _(eng):
            pe.issue(eng)


_INS = ["x", "Wq", "bq", "Wk", "bk", "Wv", "bv", "Wo", "bo"]
_FFN = ["gate_w", "gate_b", "w1", "w2"]


def kernel(**inputs):
    import numpy as _np
    import concourse.bacc as _bacc
    from concourse import mybir as _mybir
    from concourse.bass_utils import run_bass_kernel_spmd as _run

    nc = _bacc.Bacc("TRN2", target_bir_lowering=False, num_devices=1, dynamic_dma_scratch_size=1024)
    arrays, args = {}, []
    for name in ["L0_attn_" + n for n in _INS] + ["L0_ffn_" + n for n in _FFN]:
        a = _np.ascontiguousarray(inputs[name])
        arrays[f"in_{name}"] = a
        args.append(nc.dram_tensor(f"in_{name}", a.shape, _mybir.dt.from_np(a.dtype), kind="ExternalInput").ap())
    out = nc.dram_tensor("out_x", (8, 1024, 512), _mybir.dt.float32, kind="ExternalOutput").ap()
    macaron_block(nc, *args, out)
    r = _run(nc, [arrays], core_ids=[0])
    return r.results[0]["out_x"]
```
